# Optimizing a Trainium2 kernel written in Bass

```python
import numpy as np
import jax
import jax.numpy as jnp

def _softmax(x, axis=-1):
    return jax.nn.softmax(x, axis=axis)

def _gelu(x):
    return jax.nn.gelu(x, approximate=True)

def _silu(x):
    return jax.nn.silu(x)

def _sigmoid(x):
    return jax.nn.sigmoid(x)

def _layernorm(x, axis=-1, eps=1e-05):
    m = jnp.mean(x, axis=axis, keepdims=True)
    v = jnp.var(x, axis=axis, keepdims=True)
    return (x - m) / jnp.sqrt(v + eps)

def _scatter_add(tgt, idx, src, axis=0):
    return tgt.at[idx].add(src)

def _segment_sum(src, seg, n):
    return jax.ops.segment_sum(src, seg, n)
kernel_name = 'mk_adj_preln_d4_adj_r2_9343b9'

def setup_inputs(seed: int=0):
    np.random.seed(seed)
    _w = jnp.asarray

    def _rec_inputs():
        import jax
        import jax.numpy as jnp
        _gk = jax.random.key(seed)
        x = -0.0003929 + 0.9999 * jax.random.normal(jax.random.fold_in(_gk, 1), (32, 256, 512), jnp.float32)
        _a = jax.random.bernoulli(jax.random.fold_in(_gk, 2), 0.015625, (256, 256))
        _a = jnp.logical_or(_a, jnp.swapaxes(_a, -1, -2))
        _a = jnp.logical_or(_a, jnp.eye(256, dtype=bool))
        _af = _a.astype(jnp.float32)
        _af = _af * jax.random.uniform(jax.random.fold_in(_gk, 3), (256, 256), jnp.float32, 0.05, 0.198159)
        adj = _af
        return (x, adj)
    x, adj = _rec_inputs()

    def _L0_gnn_setup():
        import jax, jax.numpy as jnp
        import numpy as np
        NEG_SLOPE = 0.01
        key = jax.random.key(seed)
        k1, k2, k3, k4, k5 = jax.random.split(key, 5)
        B, C, N, O = (32, 256, 512, 256)
        x = jax.random.normal(k1, (B, C, N), dtype=jnp.float32)
        wq = jax.random.normal(k2, (C,), dtype=jnp.float32) * (1.0 / np.sqrt(C))
        wk = jax.random.normal(k3, (C,), dtype=jnp.float32) * (1.0 / np.sqrt(C))
        wm = jax.random.normal(k4, (O, C), dtype=jnp.float32) * (1.0 / np.sqrt(C))
        bm = jax.random.normal(k5, (O,), dtype=jnp.float32) * 0.01
        return {'x': x, 'wq': wq, 'wk': wk, 'wm': wm, 'bm': bm}
    _L0_gnn_all = _L0_gnn_setup()
    _L0_gnn_in = {k: v for k, v in _L0_gnn_all.items() if k in ('wq', 'wk', 'bm')}
    del _L0_gnn_all

    def _L1_gnn_setup():
        import jax, jax.numpy as jnp
        import numpy as np
        EPS = 1e-08

        def _row_stochastic_causal(A, causal_mask):
            A = A * causal_mask
            deg = jnp.maximum(A.sum(axis=-1, keepdims=True), EPS)
            return A / deg
        key = jax.random.key(seed)
        k = jax.random.split(key, 5)
        B, N, D = (4, 1024, 512)
        s = 1.0 / np.sqrt(D)
        h = jax.random.normal(k[0], (B, N, D), dtype=jnp.float32)
        W_lang = jax.random.normal(k[1], (D, D), dtype=jnp.float32) * s
        W_grav = jax.random.normal(k[2], (D, D), dtype=jnp.float32) * s
        W_V = jax.random.normal(k[3], (D, D), dtype=jnp.float32) * s
        W_O = jax.random.normal(k[4], (D, D), dtype=jnp.float32) * s
        causal_mask = jnp.tril(jnp.ones((N, N), dtype=jnp.float32))
        gate_logit = jnp.zeros((), jnp.float32)
        log_sigma = jnp.zeros((), jnp.float32)
        return {'h': h, 'causal_mask': causal_mask, 'W_lang': W_lang, 'W_grav': W_grav, 'W_V': W_V, 'W_O': W_O, 'gate_logit': gate_logit, 'log_sigma': log_sigma}
    _L1_gnn_all = _L1_gnn_setup()
    _L1_gnn_in = {k: v for k, v in _L1_gnn_all.items() if k in ('W_lang', 'W_grav', 'W_V', 'W_O', 'gate_logit', 'log_sigma')}
    del _L1_gnn_all

    def _L2_gnn_setup():
        import jax, jax.numpy as jnp
        import numpy as np
        DIM = 199
        K_HOP = 3

        def _khop_support(n, k):
            A = np.eye(n, dtype=np.float64)
            idx = np.arange(n)
            A[idx, (idx + 1) % n] = 1.0
            A[(idx + 1) % n, idx] = 1.0
            S = np.linalg.matrix_power(A, k)
            return (S > 0).astype(np.float32)
        key = jax.random.key(seed)
        kx, kk = jax.random.split(key)
        batch, n, f = (128, DIM, 512)
        x = jax.random.normal(kx, (batch, n, f), dtype=jnp.float32)
        support = jnp.asarray(_khop_support(n, K_HOP))
        limit = float(np.sqrt(6.0 / (n + n)))
        kernel = jax.random.uniform(kk, (n, n), minval=-limit, maxval=limit, dtype=jnp.float32)
        bias = jnp.zeros((f,), dtype=jnp.float32)
        return {'x': x, 'support': support, 'kernel': kernel, 'bias': bias}
    _L2_gnn_all = _L2_gnn_setup()
    _L2_gnn_in = {k: v for k, v in _L2_gnn_all.items() if k in ('bias',)}
    del _L2_gnn_all

    def _L3_gnn_setup():
        import jax, jax.numpy as jnp
        import numpy as np
        EPS = 1e-08

        def _row_stochastic_causal(A, causal_mask):
            A = A * causal_mask
            deg = jnp.maximum(A.sum(axis=-1, keepdims=True), EPS)
            return A / deg
        key = jax.random.key(seed)
        k = jax.random.split(key, 5)
        B, N, D = (4, 1024, 512)
        s = 1.0 / np.sqrt(D)
        h = jax.random.normal(k[0], (B, N, D), dtype=jnp.float32)
        W_lang = jax.random.normal(k[1], (D, D), dtype=jnp.float32) * s
        W_grav = jax.random.normal(k[2], (D, D), dtype=jnp.float32) * s
        W_V = jax.random.normal(k[3], (D, D), dtype=jnp.float32) * s
        W_O = jax.random.normal(k[4], (D, D), dtype=jnp.float32) * s
        causal_mask = jnp.tril(jnp.ones((N, N), dtype=jnp.float32))
        gate_logit = jnp.zeros((), jnp.float32)
        log_sigma = jnp.zeros((), jnp.float32)
        return {'h': h, 'causal_mask': causal_mask, 'W_lang': W_lang, 'W_grav': W_grav, 'W_V': W_V, 'W_O': W_O, 'gate_logit': gate_logit, 'log_sigma': log_sigma}
    _L3_gnn_all = _L3_gnn_setup()
    _L3_gnn_in = {k: v for k, v in _L3_gnn_all.items() if k in ('W_lang', 'W_grav', 'W_V', 'W_O', 'gate_logit', 'log_sigma')}
    del _L3_gnn_all
    return {'x': x, 'adj': adj, 'L0_gnn_wq': _L0_gnn_in['wq'], 'L0_gnn_wk': _L0_gnn_in['wk'], 'L0_gnn_bm': _L0_gnn_in['bm'], 'L1_gnn_W_lang': _L1_gnn_in['W_lang'], 'L1_gnn_W_grav': _L1_gnn_in['W_grav'], 'L1_gnn_W_V': _L1_gnn_in['W_V'], 'L1_gnn_W_O': _L1_gnn_in['W_O'], 'L1_gnn_gate_logit': _L1_gnn_in['gate_logit'], 'L1_gnn_log_sigma': _L1_gnn_in['log_sigma'], 'L2_gnn_bias': _L2_gnn_in['bias'], 'L3_gnn_W_lang': _L3_gnn_in['W_lang'], 'L3_gnn_W_grav': _L3_gnn_in['W_grav'], 'L3_gnn_W_V': _L3_gnn_in['W_V'], 'L3_gnn_W_O': _L3_gnn_in['W_O'], 'L3_gnn_gate_logit': _L3_gnn_in['gate_logit'], 'L3_gnn_log_sigma': _L3_gnn_in['log_sigma']}

def reference(x, adj, L0_gnn_wq, L0_gnn_wk, L0_gnn_bm, L1_gnn_W_lang, L1_gnn_W_grav, L1_gnn_W_V, L1_gnn_W_O, L1_gnn_gate_logit, L1_gnn_log_sigma, L2_gnn_bias, L3_gnn_W_lang, L3_gnn_W_grav, L3_gnn_W_V, L3_gnn_W_O, L3_gnn_gate_logit, L3_gnn_log_sigma):
    import jax
    import jax.numpy as jnp

    def _L0_gnn_ref(x, wq, wk, wm, bm):
        import jax, jax.numpy as jnp
        import numpy as np
        NEG_SLOPE = 0.01
        q = jnp.einsum('c,bcn->bn', wq, x)
        k = jnp.einsum('c,bcn->bn', wk, x)
        scores = q[:, None, :] + k[:, :, None]
        scores = jnp.where(scores > 0, scores, NEG_SLOPE * scores)
        att = jax.nn.softmax(scores, axis=-1)
        agg = jnp.einsum('bcn,bmn->bcm', x, att)
        out = jnp.einsum('oc,bcm->bom', wm, agg) + bm[None, :, None]
        return jax.nn.relu(out)

    def _L1_gnn_ref(h, causal_mask, W_lang, W_grav, W_V, W_O, gate_logit, log_sigma):
        import jax, jax.numpy as jnp
        import numpy as np
        EPS = 1e-08

        def _row_stochastic_causal(A, causal_mask):
            A = A * causal_mask
            deg = jnp.maximum(A.sum(axis=-1, keepdims=True), EPS)
            return A / deg
        z_l = jnp.einsum('bnd,ed->bne', h, W_lang)
        z_g = jnp.einsum('bnd,ed->bne', h, W_grav)
        v = jnp.einsum('bnd,ed->bne', h, W_V)
        N = h.shape[-2]
        not_eye = 1.0 - jnp.eye(N, dtype=h.dtype)
        zn = z_l / jnp.maximum(jnp.linalg.norm(z_l, axis=-1, keepdims=True), EPS)
        A_l = jnp.maximum(jnp.einsum('bnd,bmd->bnm', zn, zn), 0.0) * not_eye
        sq = jnp.sum(z_g * z_g, axis=-1, keepdims=True)
        d2 = jnp.maximum(sq + jnp.swapaxes(sq, -1, -2) - 2.0 * jnp.einsum('bnd,bmd->bnm', z_g, z_g), 0.0)
        sigma = jnp.exp(log_sigma)
        A_g = jnp.exp(-d2 / (2.0 * sigma * sigma)) * not_eye
        K_l = _row_stochastic_causal(A_l, causal_mask)
        K_g = _row_stochastic_causal(A_g, causal_mask)
        w_l = jax.nn.sigmoid(gate_logit)
        K = w_l * K_l + (1.0 - w_l) * K_g
        out = jnp.einsum('bnm,bmd->bnd', K, v)
        return jnp.einsum('bnd,ed->bne', out, W_O)

    def _L2_gnn_ref(x, support, kernel, bias):
        import jax, jax.numpy as jnp
        import numpy as np
        DIM = 199
        K_HOP = 3

        def _khop_support(n, k):
            A = np.eye(n, dtype=np.float64)
            idx = np.arange(n)
            A[idx, (idx + 1) % n] = 1.0
            A[(idx + 1) % n, idx] = 1.0
            S = np.linalg.matrix_power(A, k)
            return (S > 0).astype(np.float32)
        W = support * kernel
        out = jnp.einsum('bnf,nm->bmf', x, W)
        out = out + bias
        return out

    def _L3_gnn_ref(h, causal_mask, W_lang, W_grav, W_V, W_O, gate_logit, log_sigma):
        import jax, jax.numpy as jnp
        import numpy as np
        EPS = 1e-08

        def _row_stochastic_causal(A, causal_mask):
            A = A * causal_mask
            deg = jnp.maximum(A.sum(axis=-1, keepdims=True), EPS)
            return A / deg
        z_l = jnp.einsum('bnd,ed->bne', h, W_lang)
        z_g = jnp.einsum('bnd,ed->bne', h, W_grav)
        v = jnp.einsum('bnd,ed->bne', h, W_V)
        N = h.shape[-2]
        not_eye = 1.0 - jnp.eye(N, dtype=h.dtype)
        zn = z_l / jnp.maximum(jnp.linalg.norm(z_l, axis=-1, keepdims=True), EPS)
        A_l = jnp.maximum(jnp.einsum('bnd,bmd->bnm', zn, zn), 0.0) * not_eye
        sq = jnp.sum(z_g * z_g, axis=-1, keepdims=True)
        d2 = jnp.maximum(sq + jnp.swapaxes(sq, -1, -2) - 2.0 * jnp.einsum('bnd,bmd->bnm', z_g, z_g), 0.0)
        sigma = jnp.exp(log_sigma)
        A_g = jnp.exp(-d2 / (2.0 * sigma * sigma)) * not_eye
        K_l = _row_stochastic_causal(A_l, causal_mask)
        K_g = _row_stochastic_causal(A_g, causal_mask)
        w_l = jax.nn.sigmoid(gate_logit)
        K = w_l * K_l + (1.0 - w_l) * K_g
        out = jnp.einsum('bnm,bmd->bnd', K, v)
        return jnp.einsum('bnd,ed->bne', out, W_O)
    h = jnp.maximum(_layernorm(x, axis=-1), 0.0)
    x = x + _L0_gnn_ref(h, L0_gnn_wq, L0_gnn_wk, adj, L0_gnn_bm)
    h = jnp.maximum(_layernorm(x, axis=-1), 0.0)
    x = x + _L1_gnn_ref(h, adj, L1_gnn_W_lang, L1_gnn_W_grav, L1_gnn_W_V, L1_gnn_W_O, L1_gnn_gate_logit, L1_gnn_log_sigma)
    h = jnp.maximum(_layernorm(x, axis=-1), 0.0)
    x = x + _L2_gnn_ref(h, adj, adj, L2_gnn_bias)
    h = jnp.maximum(_layernorm(x, axis=-1), 0.0)
    x = x + _L3_gnn_ref(h, adj, L3_gnn_W_lang, L3_gnn_W_grav, L3_gnn_W_V, L3_gnn_W_O, L3_gnn_gate_logit, L3_gnn_log_sigma)
    return x

_drawn_inputs = setup_inputs


def setup_inputs(seed=0):
    import zlib

    import numpy as np

    out = dict(_drawn_inputs(seed))
    spreads = {'L2_gnn_bias': (0.0, 0.1)}
    factors = {'L0_gnn_wq': 8.0,
     'L0_gnn_wk': 8.0,
     'L0_gnn_bm': 7.303,
     'L1_gnn_W_lang': 5.884,
     'L3_gnn_W_lang': 6.921}
    for name, (base, spread) in spreads.items():
        noise = np.random.default_rng([zlib.crc32(name.encode()), seed]).standard_normal(out[name].shape)
        drawn = base * np.exp(spread * noise) if base else spread * noise
        out[name] = jnp.asarray(drawn.astype(out[name].dtype))
    for name, factor in factors.items():
        out[name] = (out[name] * factor).astype(out[name].dtype)
    return out
```

```python
from contextlib import ExitStack

import concourse.bass as bass
from concourse import mybir

F32 = mybir.dt.float32
F16 = mybir.dt.float16
U32 = mybir.dt.uint32
ALU = mybir.AluOpType
ACT = mybir.ActivationFunctionType
AX_X = mybir.AxisListType.X

P = 128
CHAIN_SQUARE = 37
DVE_STEPS, ACT_STEPS, POOL_STEPS = 24, 1, 1
LN_EPS = 1e-5
EPS = 1e-8
SLOPE = 0.01

H_SCALE = 256.0
W_TOP = 8.0
PT_SCALE = 0.5
E_SCALE = 16384.0
K_SCALE = 1024.0

BIG_WITH_L0 = [("Zl", 0), ("Zl", 1), ("P1", None), ("Zg", 0), ("P2", None), ("Zg", 1), ("Gl", None),
               ("P3", None), ("Gg", None), ("P4a", None), ("Rl", None), ("V", 0), ("P4b", None),
               ("Rg", None), ("V", 1), ("KT", None), ("T", None), ("Y", None)]
TAIL_STAGES = ("Zl", "Zg", "Gl", "Gg", "Rl", "Rg", "V", "KT", "Y")


def orders():
    first = [(0, "N0", 0, None)]
    for stage, half in BIG_WITH_L0:
        if stage in TAIL_STAGES:
            first.append((1, stage, 3, half))
        else:
            first.append((0, stage, 1 if stage == "T" else 0, half))
        if stage == "P4b":
            first.append((0, "N1", 1, None))
    tail = [s for s in first if s[0] == 1]
    head = [s for s in first if s[0] == 0]
    rest = [(1, "N0", 0, None), (0, "Zl", 1, 0), (1, "P1", 0, None), (0, "Zl", 1, 1), (0, "Zg", 1, 0),
            (1, "P2", 0, None), (0, "Zg", 1, 1), (1, "P3", 0, None), (0, "Gl", 1, None), (1, "P4a", 0, None),
            (0, "Gg", 1, None), (1, "P4b", 0, None), (1, "N1", 1, None), (0, "Rl", 1, None), (0, "V", 1, 0),
            (0, "Rg", 1, None), (0, "V", 1, 1), (0, "KT", 1, None), (1, "T", 1, None), (0, "Y", 1, None),
            (0, "N2", 2, None),
            (1, "Zl", 1, 0), (1, "Zl", 1, 1), (1, "Zg", 1, 0), (0, "Y2", 2, None), (0, "N3", 3, None),
            (1, "Zg", 1, 1), (1, "Gl", 1, None), (1, "Gg", 1, None), (1, "Rl", 1, None), (1, "V", 1, 0),
            (1, "Rg", 1, None), (1, "V", 1, 1), (1, "KT", 1, None), (0, "T", 3, None), (1, "Y", 1, None),
            (1, "N2", 2, None),
            (0, "Zl", 3, 0), (0, "Zl", 3, 1), (0, "Zg", 3, 0), (1, "Y2", 2, None), (1, "N3", 3, None),
            (0, "Zg", 3, 1), (0, "Gl", 3, None), (0, "Gg", 3, None), (0, "Rl", 3, None), (0, "V", 3, 0),
            (0, "Rg", 3, None), (0, "V", 3, 1), (0, "KT", 3, None), (1, "T", 3, None), (0, "Y", 3, None)]
    return first, tail, head, rest


class Signal:

    def __init__(self, ctx, nc, name, per, unit=1):
        self.sems = [ctx.enter_context(nc.semaphore(f"{name}_{'ab'[s]}")) for s in range(2)]
        self.per, self.unit = per, unit

    def __getitem__(self, slot):
        return self.sems[slot]

    def at(self, sample, n):
        return sample * (self.per * self.unit) + n * self.unit


class Chain(Signal):

    def __init__(self, ctx, nc, name, per):
        super().__init__(ctx, nc, name, per)
        self.n = [0, 0]

    def link(self, eng, ins, slot, sample):
        self.n[slot] += 1
        ins.then_inc(self[slot], 1)
        eng.wait_ge(self[slot], self.at(sample, self.n[slot]))

    def end_sample(self, slot):
        assert self.n[slot] == self.per, (self.n[slot], self.per)
        self.n[slot] = 0


def later(sample):
    return not isinstance(sample, int) or sample > 0


def build(nc, x, adj, wq, wk, bm, w_lang1, w_grav1, w_v1, w_o1, gate1, sigma1, bias2,
          w_lang3, w_grav3, w_v3, w_o3, gate3, sigma3, out):
    B, C, N = x.shape
    CT, NT, DT = C // P, N // P, N // P
    PAIRS = B // 2
    x_dram = x.rearrange("b (t p) n -> b p t n", p=P)
    out_dram = out.rearrange("b (t p) n -> b p t n", p=P)

    with ExitStack() as ctx:
        def sb(name, shape, dt=F32):
            return ctx.enter_context(nc.sbuf_tensor(name, shape, dt))

        def one(name):
            return ctx.enter_context(nc.semaphore(name))

        def signal(name, per, unit=1):
            return Signal(ctx, nc, name, per, unit)

        ident = sb("ident", [P, P])
        ones = sb("ones", [P, 1])
        minus_half = sb("minus_half", [P, CT])
        adj_sb = sb("adj_sb", [P, CT, C])
        adj_off = sb("adj_off", [P, CT, C])
        adjT = [sb(f"adjT_{p}", [P, CT, C], F16) for p in "hl"]
        adj2 = [sb(f"adj2_{p}", [P, CT, C], F16) for p in "hl"]
        wqk_f = sb("wqk_f", [P, CT, 2])
        wqk = [sb(f"wqk_{p}", [P, CT, 2], F16) for p in "hl"]
        bm_col = sb("bm_col", [P, CT])
        bias_row = sb("bias_row", [P, N])
        weight = {}
        for layer in (1, 3):
            for name in ("lang", "grav", "vo"):
                weight[name, layer] = [sb(f"w_{name}{layer}_{p}", [P, DT, N], F16) for p in "hl"]
        MATS = ["lang1", "grav1", "vo1", "lang3", "grav3", "vo3", "adj", "qk"]
        scale = sb("scale", [P, len(MATS), 1])
        inv = sb("inv", [P, len(MATS), 1])
        absmax = sb("absmax", [P, 5])

        def s_of(name):
            return scale[:, MATS.index(name), :]

        def i_of(name):
            return inv[:, MATS.index(name), :]

        qk_unscale = sb("qk_unscale", [P, 1])
        l0_unscale = sb("l0_unscale", [P, 1])
        l2_unscale = sb("l2_unscale", [P, 1])
        gates = sb("gates", [P, 2, 2])
        norm_floor = sb("norm_floor", [P, 2])
        two_c = sb("two_c", [P, 2])
        neg_c = sb("neg_c", [P, 2])
        v_unscale = sb("v_unscale", [P, 2])
        gl = sb("gl", [P, 4])
        small = sb("small", [P, 8])

        def both(name, shape, dt=F32):
            return [sb(f"{name}_{c}", shape, dt) for c in "ab"]

        def both2(name, shape):
            return [[sb(f"{name}{p}_{c}", shape, F16) for p in "hl"] for c in "ab"]

        xin = both("xin", [P, CT, N])
        xs = both("xs", [P, CT, N])
        t_ln = both("t_ln", [P, CT, N])
        xb = both("xb", [P, CT, N])
        stats = both("stats", [P, CT, 6])
        mv = both("mv", [P, CT, 2])
        var_in = both("var_in", [P, CT])
        rstd = both("rstd", [P, CT])
        h = both2("h", [P, CT, N])
        PT = both2("PT", [P, NT, C])
        qk = both("qk", [P, NT, 2])
        qm = both("qm", [P, 1])
        Q = both("Q", [P, 1])
        nQ = both("nQ", [P, 1])
        qd = both("qd", [P, NT])
        ea = both("ea", [P, NT])
        eb = both("eb", [P, NT])
        r12 = both("r12", [P, 2, N])
        uv = both("uv", [P, 2, N])
        tmp = sb("tmp", [P, 2, N])
        E = both("E", [P, NT, N])
        E16 = both2("E", [P, NT, N])
        esum = both("esum", [P, 2, N])
        rs0 = both("rs0", [P, NT])
        rsx = both("rsx", [P, N])
        orl = r12
        hT = both2("hT", [P, DT, C])
        zl = both2("zl", [P, DT, C])
        zg = both2("zg", [P, DT, C])
        vv = [[e[:, 0:CT, :] for e in E16[s]] for s in range(2)]
        KT = [[e[:, CT, :].rearrange("p (t c) -> p t c", t=CT) for e in E16[s]] for s in range(2)]

        def tile_of(buf, n):
            return [buf[s][:, n, :].rearrange("p (t c) -> p t c", t=CT) for s in range(2)]

        diag = both("diag", [P, 2, CT, P])
        carry = both("carry", [P, 1])
        dgl = both("dgl", [P, CT])
        dgg = both("dgg", [P, CT])
        nrm = both("nrm", [P, CT])
        rsl = both("rsl", [P, CT])
        bg = both("bg", [P, CT])
        sqr = both("sqr", [P, C])
        tl = tile_of(E, 0)
        Bl = tile_of(E, 1)
        e0 = tile_of(E, 2)
        Eg = tile_of(E, 3)
        Bg = tile_of(xb, 0)
        deg = both("deg", [P, 2, CT])
        rdeg = both("rdeg", [P, 2, CT])
        Km = tile_of(xb, 1)
        bank = [[ctx.enter_context(nc.psum_tensor(f"bank{b}_{c}", [P, 512], F32)) for b in range(4)]
                for c in "ab"]

        xin_landed = signal("xin_landed", 1, 16)
        x_stored = signal("x_stored", 1, 16)
        x1_done = signal("x1_done", 2)
        x2_done = signal("x2_done", 2)
        x4_done = signal("x4_done", 2)
        xb_done = signal("xb_done", 2)
        stats_done = signal("stats_done", 4)
        rstd_done = signal("rstd_done", 4)
        t_done = signal("t_done", 8)
        hh_done = signal("hh_done", 4)
        hl_done = signal("hl_done", 4)
        pt_done = signal("pt_done", 2)
        pth_done = signal("pth_done", 2)
        ptl_done = signal("ptl_done", 2)
        qk_done = signal("qk_done", 1)
        qkc_done = signal("qkc_done", 1)
        qm_done = signal("qm_done", 1)
        qmr_done = signal("qmr_done", 1)
        Q_done = signal("Q_done", 1)
        uv_done = signal("uv_done", 1)
        e_done = signal("e_done", 4)
        eh_done = signal("eh_done", 4)
        el_done = signal("el_done", 4)
        esum_done = signal("esum_done", 1)
        out_done = signal("out_done", 1)
        scol_done = signal("scol_done", 1)
        rs0_done = signal("rs0_done", 1)
        rsr_done = signal("rsr_done", 1)
        rsx_done = signal("rsx_done", 1)
        om_done = signal("om_done", 2)
        orl_done = signal("orl_done", 2)
        hT_ps = signal("hT_ps", 4)
        hTh_done = signal("hTh_done", 4)
        hTl_done = signal("hTl_done", 4)
        z_ps = signal("z_ps", 8)
        zh_done = signal("zh_done", 8)
        zlo_done = signal("zlo_done", 8)
        gl_ps = signal("gl_ps", 2)
        gg_ps = signal("gg_ps", 2)
        dgl_done = signal("dgl_done", 2)
        dgg_done = signal("dgg_done", 2)
        rsl_done = signal("rsl_done", 2)
        bg_done = signal("bg_done", 2)
        rl_ps = signal("rl_ps", 2)
        row_used = signal("row_used", 2)
        rg_ps = signal("rg_ps", 2)
        sqr_done = signal("sqr_done", 2)
        tl_done = signal("tl_done", 2)
        e0_done = signal("e0_done", 2)
        eg_done = signal("eg_done", 2)
        rdeg_done = signal("rdeg_done", 2)
        kg_done = signal("kg_done", 2)
        K_done = signal("K_done", 2)
        v_ps = signal("v_ps", 4)
        vh_done = signal("vh_done", 4)
        vl_done = signal("vl_done", 4)
        kt_ps = signal("kt_ps", 2)
        kth_done = signal("kth_done", 2)
        ktl_done = signal("ktl_done", 2)
        y_ps = signal("y_ps", 6)
        dve_chain = Chain(ctx, nc, "dve_chain", DVE_STEPS)
        act_chain = Chain(ctx, nc, "act_chain", ACT_STEPS)
        pool_chain = Chain(ctx, nc, "pool_chain", POOL_STEPS)

        staging = [E[0], E[1]]
        wo_t = [t_ln[0], t_ln[1]]
        w_landed = [one("w_landed_0"), one("w_landed_1")]
        c_landed = one("c_landed")
        consts_made = one("consts_made")
        w_read = one("w_read")
        max_found = one("max_found")
        max_row = one("max_row")
        scaled = one("scaled")
        product = one("product")
        w_hi = one("w_hi")
        w_lo = one("w_lo")
        prep_exp = one("prep_exp")
        prep_chain = one("prep_chain")
        jobs = []
        for layer, wl, wg, wo, wv in ((1, w_lang1, w_grav1, w_o1, w_v1), (3, w_lang3, w_grav3, w_o3, w_v3)):
            jobs += [(f"lang{layer}", wl, "turn", ("lang", layer)), (f"grav{layer}", wg, "turn", ("grav", layer)),
                     (None, wo, "keep", None), (f"vo{layer}", wv, "multiply", ("vo", layer))]
        total, upto = [0, 0, 0], []
        for _, _, how, _ in jobs:
            total = [total[0] + (how != "keep"), total[1] + 4, total[2] + 4 * (how != "keep")]
            upto.append(tuple(total))

        with nc.Block() as prep:
            @prep.sync
            def _(sp):
                with nc.allow_non_contiguous_dma(reason="a few small vectors"):
                    sp.dma_start(adj_sb[:], adj.rearrange("(t p) m -> p t m", p=P)).then_inc(c_landed, 16)
                    sp.dma_start(wqk_f[:, :, 0], wq.rearrange("(t p) -> p t", p=P)).then_inc(c_landed, 16)
                    sp.dma_start(wqk_f[:, :, 1], wk.rearrange("(t p) -> p t", p=P)).then_inc(c_landed, 16)
                    sp.dma_start(bm_col[:], bm.rearrange("(t p) -> p t", p=P)).then_inc(c_landed, 16)
                    sp.dma_start(bias_row[:], bias2.partition_broadcast(P)).then_inc(c_landed, 16)
                    for k, a in enumerate((gate1, gate3, sigma1, sigma3)):
                        sp.dma_start(gl[:, k:k + 1], a.to_broadcast((P, 1))).then_inc(c_landed, 16)
                for k, (_, w, _, _) in enumerate(jobs):
                    if k >= 2:
                        sp.wait_ge(w_read, k - 1)
                    sp.dma_start(staging[k % 2][:], w.rearrange("(t p) n -> p t n", p=P)).then_inc(w_landed[k % 2], 16)

            @prep.gpsimd
            def _(pool):
                pool.memset(ident[:], 0.0).then_inc(consts_made, 1)
                pool.memset(ones[:], 1.0).then_inc(consts_made, 1)
                pool.memset(minus_half[:], -0.5).then_inc(consts_made, 1)
                pool.wait_ge(consts_made, 3)
                pool.affine_select(out=ident[:], in_=ident[:], compare_op=ALU.not_equal, fill=1.0, base=0,
                                   pattern=[[-1, P]], channel_multiplier=1).then_inc(consts_made, 1)
                pool.wait_ge(c_landed, 16 * 9)
                pool.affine_select(out=adj_off[:], in_=adj_sb[:], compare_op=ALU.not_equal, fill=0.0, base=0,
                                   pattern=[[P, CT], [-1, C]], channel_multiplier=1).then_inc(consts_made, 1)

            @prep.tensor
            def _(pe):
                pe.wait_ge(consts_made, 4)
                for k, (name, _, how, _) in enumerate(jobs):
                    g = k % 2
                    if k >= 2:
                        pe.wait_ge(w_hi, upto[k - 2][1])
                        pe.wait_ge(w_lo, upto[k - 2][2])
                    if how == "turn":
                        pe.wait_ge(max_found, upto[k][0])
                        pe.transpose(bank[g][0][:, 0:P], absmax[:, 4:5].to_broadcast((P, P)), ident[:]).then_inc(max_row, 1)
                        pe.wait_ge(scaled, upto[k][0])
                    elif k:
                        pe.wait_ge(scaled, upto[k - 1][0])
                    pe.wait_ge(w_landed[k % 2], 16 * (k // 2 + 1))
                    if how == "multiply":
                        pe.wait_ge(w_hi, upto[k - 1][1])
                        for dt in range(DT):
                            for kt in range(DT):
                                mm = pe.matmul(bank[g][dt][:], staging[k % 2][:, kt, dt * P:(dt + 1) * P],
                                               wo_t[kt // 2][:, kt % 2, :], start=kt == 0, stop=kt == DT - 1)
                        mm.then_inc(product, 1)
                        pe.wait_ge(max_found, upto[k][0])
                        pe.transpose(bank[1 - g][0][:, 0:P], absmax[:, 4:5].to_broadcast((P, P)),
                                     ident[:]).then_inc(max_row, 1)
                        pe.wait_ge(max_row, upto[k][0])
                        pe.nop().then_inc(w_read, 1)
                    else:
                        for dt in range(DT):
                            for et in range(DT):
                                mm = pe.transpose(bank[g][dt][:, et * P:(et + 1) * P],
                                                  staging[k % 2][:, et, dt * P:(dt + 1) * P], ident[:])
                        mm.then_inc(product, 1)
                        pe.wait_ge(product, k + 1)
                        pe.nop().then_inc(w_read, 1)
                pe.wait_ge(w_hi, upto[-1][1])
                pe.wait_ge(w_lo, upto[-1][2])
                for ct in range(CT):
                    for ot in range(CT):
                        mm = pe.transpose(bank[0][0][:, ct * C + ot * P:ct * C + (ot + 1) * P],
                                          adj_sb[:, ot, ct * P:(ct + 1) * P], ident[:])
                mm.then_inc(product, 1)
                for n in range(2):
                    pe.wait_ge(max_found, upto[-1][0] + n + 1)
                    pe.transpose(bank[1][n][:, 0:P], absmax[:, 4:5].to_broadcast((P, P)), ident[:]).then_inc(max_row, 1)

            @prep.scalar
            def _(act):
                act.wait_ge(c_landed, 16 * 9)
                act.activation(small[:, 0:2], gl[:, 0:2], ACT.Exp, scale=-1.0).then_inc(prep_exp, 1)
                act.activation(small[:, 2:4], gl[:, 2:4], ACT.Exp).then_inc(prep_exp, 1)
                for k, (name, _, how, key) in enumerate(jobs):
                    act.wait_ge(product, k + 1)
                    act.wait_ge(scaled, upto[k][0])
                    for dt in range(DT):
                        if how == "keep":
                            a = act.activation(wo_t[dt // 2][:, dt % 2, :], bank[k % 2][dt][:], ACT.Copy)
                        else:
                            a = act.activation(weight[key][0][:, dt, :], bank[k % 2][dt][:], ACT.Copy, scale=s_of(name))
                        a.then_inc(w_hi, 1)
                n = upto[-1][1]
                act.wait_ge(product, len(jobs) + 1)
                act.wait_ge(scaled, upto[-1][0] + 1)
                act.activation(adjT[0][:], bank[0][0][:], ACT.Copy, scale=s_of("adj")).then_inc(w_hi, 1)
                act.wait_ge(prep_chain, CHAIN_SQUARE)
                act.activation(adj2[0][:], tl[0][:], ACT.Copy).then_inc(w_hi, 1)
                act.wait_ge(scaled, upto[-1][0] + 2)
                act.activation(wqk[0][:], wqk_f[:], ACT.Copy, scale=s_of("qk")).then_inc(w_hi, 1)

            @prep.vector
            def _(dve):
                steps = [0]

                def link(ins):
                    steps[0] += 1
                    ins.then_inc(prep_chain, 1)
                    dve.wait_ge(prep_chain, steps[0])

                def find_scale(name, src_group, src_bank, nth):
                    dve.wait_ge(max_row, nth)
                    link(dve.tensor_reduce(small[:, 4:5], bank[src_group][src_bank][:, 0:P], AX_X, ALU.max))
                    link(dve.tensor_scalar(small[:, 5:6].bitcast(U32), small[:, 4:5].bitcast(U32), 0x7F800000, None,
                                           ALU.bitwise_and))
                    link(dve.tensor_scalar(small[:, 6:7], small[:, 5:6], 2.0 ** -100, 1.0 / W_TOP, ALU.max, ALU.mult))
                    link(dve.tensor_copy(i_of(name), small[:, 6:7]))
                    dve.reciprocal(s_of(name), small[:, 6:7]).then_inc(scaled, 1)
                    dve.wait_ge(scaled, nth)

                found = [0]

                def find_max(parts):
                    for n, a in enumerate(parts):
                        last = dve.tensor_reduce(absmax[:, n:n + 1], a, AX_X, ALU.max, apply_absolute_value=True)
                    link(last)
                    dve.tensor_reduce(absmax[:, 4:5], absmax[:, 0:len(parts)], AX_X, ALU.max).then_inc(max_found, 1)
                    found[0] += 1
                    return found[0]

                for k, (name, _, how, key) in enumerate(jobs):
                    g = k % 2
                    if how == "keep":
                        continue
                    if how == "turn":
                        dve.wait_ge(w_landed[k % 2], 16 * (k // 2 + 1))
                        nth = find_max([staging[k % 2][:, t, :] for t in range(DT)])
                        find_scale(name, g, 0, nth)
                    else:
                        dve.wait_ge(product, k + 1)
                        nth = find_max([bank[g][dt][:] for dt in range(DT)])
                        find_scale(name, 1 - g, 0, nth)
                    for dt in range(DT):
                        dve.wait_ge(w_hi, upto[k][1] - DT + dt + 1)
                        dve.scalar_tensor_tensor(weight[key][1][:, dt, :], bank[g][dt][:], s_of(name),
                                                 weight[key][0][:, dt, :], ALU.mult, ALU.subtract).then_inc(w_lo, 1)
                dve.wait_ge(c_landed, 16 * 9)
                nth = find_max([adj_sb[:, t, :] for t in range(CT)])
                find_scale("adj", 1, 0, nth)
                link(dve.tensor_scalar(Bl[0][:], adj_sb[:], s_of("adj"), None, ALU.mult))
                link(dve.tensor_tensor(tl[0][:], Bl[0][:], Bl[0][:], ALU.mult))
                assert steps[0] == CHAIN_SQUARE, steps[0]
                dve.wait_ge(w_hi, upto[-1][1] + 1)
                dve.scalar_tensor_tensor(adjT[1][:], bank[0][0][:].rearrange("p (t c) -> p t c", t=CT), s_of("adj"),
                                         adjT[0][:], ALU.mult, ALU.subtract)
                dve.wait_ge(w_hi, upto[-1][1] + 2)
                dve.tensor_tensor(adj2[1][:], tl[0][:], adj2[0][:], ALU.subtract)
                nth = find_max([wqk_f[:, t, :] for t in range(CT)])
                find_scale("qk", 1, 1, nth)
                dve.wait_ge(w_hi, upto[-1][1] + 3)
                dve.scalar_tensor_tensor(wqk[1][:], wqk_f[:], s_of("qk"), wqk[0][:], ALU.mult, ALU.subtract)
                dve.tensor_scalar(qk_unscale[:], i_of("qk"), 1.0 / H_SCALE, None, ALU.mult)
                dve.tensor_scalar(l0_unscale[:], i_of("adj"), 1.0 / (PT_SCALE * E_SCALE), None, ALU.mult)
                dve.scalar_tensor_tensor(l2_unscale[:], i_of("adj"), 1.0 / H_SCALE, i_of("adj"), ALU.mult, ALU.mult)
                dve.wait_ge(prep_exp, 2)
                for li, layer in enumerate((1, 3)):
                    col = slice(li, li + 1)
                    link(dve.tensor_scalar(small[:, 4:5], small[:, col], 1.0, None, ALU.add))
                    link(dve.reciprocal(small[:, 5:6], small[:, 4:5]))
                    dve.tensor_scalar(gates[:, li, 0:1], small[:, 5:6], K_SCALE, None, ALU.mult)
                    dve.tensor_scalar(gates[:, li, 1:2], small[:, 5:6], -K_SCALE, K_SCALE, ALU.mult, ALU.add)
                    sigma = small[:, 2 + li:3 + li]
                    link(dve.scalar_tensor_tensor(small[:, 6:7], sigma, 1.0, sigma, ALU.mult, ALU.mult))
                    link(dve.reciprocal(small[:, 7:8], small[:, 6:7]))
                    ig = i_of(f"grav{layer}")
                    link(dve.scalar_tensor_tensor(small[:, 6:7], ig, small[:, 7:8], ig, ALU.mult, ALU.mult))
                    dve.tensor_scalar(two_c[:, col], small[:, 6:7], 1.0, None, ALU.mult)
                    dve.tensor_scalar(neg_c[:, col], small[:, 6:7], -0.5, None, ALU.mult)
                    sl = s_of(f"lang{layer}")
                    dve.scalar_tensor_tensor(norm_floor[:, col], sl, EPS * EPS, sl, ALU.mult, ALU.mult)
                    dve.tensor_scalar(v_unscale[:, col], i_of(f"vo{layer}"), 1.0 / K_SCALE, None, ALU.mult)

        first, tail, head, rest = orders()

        def run(eng, stages):
            def some(order, i):
                for slot, stage, layer, half in order:
                    behind = 1 if (order is first or order is tail) and slot == 1 else 0
                    name = stage[0] if stage in ("N0", "N1", "N2", "N3") else stage
                    if name in stages:
                        stages[name](slot, i - behind, layer, half)
            some(head, 0)
            some(rest, 0)
            with eng.Fori(1, PAIRS) as i:
                some(first, i)
                some(rest, i)
            some(tail, PAIRS)

        block = ctx.enter_context(nc.Block())

        @block.sync
        def _(sp):
            def load(slot, j, *_):
                if later(j):
                    sp.wait_ge(x1_done[slot], x1_done.at(j, 0))
                sp.dma_start(xin[slot][:], x_dram[2 * j + slot]).then_inc(xin_landed[slot], 16)

            run(sp, {"N": lambda slot, j, layer, half: load(slot, j) if layer == 0 else None})

        @block.tensor
        def _(pe):
            hi_lo = ((0, 0), (0, 1), (1, 0))

            def p1(s, j, *_):
                if later(j):
                    pe.wait_ge(x4_done[s], x4_done.at(j, 0))
                pe.wait_ge(hl_done[s], hl_done.at(j, 2))
                for nt in range(NT):
                    o = bank[s][nt // 2][:, (nt % 2) * C:(nt % 2 + 1) * C]
                    qo = bank[s][2][:, 2 * nt:2 * nt + 2]
                    for ct in range(CT):
                        for a, b in hi_lo:
                            lhs = h[s][a][:, ct, nt * P:(nt + 1) * P]
                            k = (ct == 0 and (a, b) == (0, 0), ct == CT - 1 and (a, b) == (1, 0))
                            mm = pe.matmul(o, lhs, adjT[b][:, ct, :], start=k[0], stop=k[1])
                            mq = pe.matmul(qo, lhs, wqk[b][:, ct, :], start=k[0], stop=k[1])
                    if nt % 2 == 1:
                        mm.then_inc(pt_done[s], 1)
                mq.then_inc(qk_done[s], 1)

            def p2(s, j, *_):
                pe.wait_ge(qm_done[s], qm_done.at(j, 1))
                pe.transpose(bank[s][2][:, P:2 * P], qm[s][:, 0:1].to_broadcast((P, P)), ident[:])
                for nt in range(NT):
                    mm = pe.transpose(bank[s][3][:, nt * P:(nt + 1) * P],
                                      qk[s][:, nt, 1:2].to_broadcast((P, P)), ident[:])
                mm.then_inc(qmr_done[s], 1)

            def p3(s, j, *_):
                for nt in range(NT):
                    if nt % 2 == 0:
                        pe.wait_ge(ptl_done[s], ptl_done.at(j, nt // 2 + 1))
                    pe.wait_ge(el_done[s], el_done.at(j, nt + 1))
                    for ot in range(CT):
                        for a, b in hi_lo:
                            mm = pe.matmul(bank[s][ot][:], PT[s][a][:, nt, ot * P:(ot + 1) * P],
                                           E16[s][b][:, nt, :], start=(nt == 0 and (a, b) == (0, 0)),
                                           stop=(nt == NT - 1 and (a, b) == (1, 0)))
                mm.then_inc(out_done[s], 1)

            def p4a(s, j, *_):
                pe.wait_ge(esum_done[s], esum_done.at(j, 1))
                for mt in range(NT):
                    mm = pe.matmul(bank[s][2][:, mt:mt + 1], esum[s][:, 0, mt * P:(mt + 1) * P], ones[:],
                                   start=True, stop=True)
                mm.then_inc(scol_done[s], 1)

            def p4b(s, j, *_):
                pe.wait_ge(rs0_done[s], rs0_done.at(j, 1))
                for mt in range(NT):
                    mm = pe.transpose(bank[s][3][:, mt * P:(mt + 1) * P],
                                      rs0[s][:, mt:mt + 1].to_broadcast((P, P)), ident[:])
                mm.then_inc(rsr_done[s], 1)

            def transposes(s, j, layer, _):
                for ct in range(CT):
                    pe.wait_ge(t_done[s], t_done.at(j, 2 * layer + ct + 1))
                for dt in range(DT):
                    for ct in range(CT):
                        mm = pe.transpose(bank[s][dt // 2][:, (dt % 2) * C + ct * P:(dt % 2) * C + (ct + 1) * P],
                                          t_ln[s][:, ct, dt * P:(dt + 1) * P], ident[:])
                    if dt % 2 == 1:
                        mm.then_inc(hT_ps[s], 1)

            def project(which):
                def stage(s, j, layer, half):
                    li = layer // 2
                    if which == "lang" and half == 0:
                        pe.wait_ge(hTl_done[s], hTl_done.at(j, 2 * li + 2))
                    w = weight[which, layer]
                    b0 = 2 if which == "lang" else 0
                    for e in (0, 1):
                        et = 2 * half + e
                        for dt in range(DT):
                            for a, b in hi_lo:
                                mm = pe.matmul(bank[s][b0 + half][:, e * C:(e + 1) * C],
                                               w[a][:, dt, et * P:(et + 1) * P], hT[s][b][:, dt, :],
                                               start=(dt == 0 and (a, b) == (0, 0)),
                                               stop=(dt == DT - 1 and (a, b) == (1, 0)))
                    mm.then_inc(z_ps[s], 1)
                return stage

            def gram(which):
                def stage(s, j, layer, _):
                    li = layer // 2
                    z, b0, k, done = (zl, 2, 2, gl_ps) if which == "lang" else (zg, 3, 4, gg_ps)
                    pe.wait_ge(zlo_done[s], zlo_done.at(j, 4 * li + k))
                    for nt in range(CT):
                        for et in range(DT):
                            for a, b in hi_lo:
                                mm = pe.matmul(bank[s][b0][:, nt * C:(nt + 1) * C],
                                               z[s][a][:, et, nt * P:(nt + 1) * P], z[s][b][:, et, :],
                                               start=(et == 0 and (a, b) == (0, 0)),
                                               stop=(et == DT - 1 and (a, b) == (1, 0)))
                    mm.then_inc(done[s], 1)
                return stage

            def rows(which):
                def stage(s, j, layer, _):
                    li = layer // 2
                    src, c0, ready, done = ((rsl, 0, rsl_done, rl_ps) if which == "lang"
                                            else (dgg, C, dgg_done, rg_ps))
                    pe.wait_ge(ready[s], ready.at(j, li + 1))
                    if which == "grav":
                        pe.wait_ge(row_used[s], row_used.at(j, li + 1))
                    for mt in range(CT):
                        mm = pe.transpose(bank[s][0][:, c0 + mt * P:c0 + (mt + 1) * P],
                                          src[s][:, mt:mt + 1].to_broadcast((P, P)), ident[:])
                    mm.then_inc(done[s], 1)
                return stage

            def values(s, j, layer, half):
                if half == 1:
                    pe.wait_ge(tl_done[s], tl_done.at(j, layer // 2 + 1))
                w = weight["vo", layer]
                for dt in range(DT):
                    for a, b in hi_lo:
                        mm = pe.matmul(bank[s][1 + half][:], hT[s][a][:, dt, half * P:(half + 1) * P], w[b][:, dt, :],
                                       start=(dt == 0 and (a, b) == (0, 0)), stop=(dt == DT - 1 and (a, b) == (1, 0)))
                mm.then_inc(v_ps[s], 1)

            def mixture_t(s, j, layer, _):
                pe.wait_ge(K_done[s], K_done.at(j, layer // 2 + 1))
                for mt in range(CT):
                    for nt in range(CT):
                        mm = pe.transpose(bank[s][3][:, mt * C + nt * P:mt * C + (nt + 1) * P],
                                          Km[s][:, nt, mt * P:(mt + 1) * P], ident[:])
                mm.then_inc(kt_ps[s], 1)

            def apply(s, j, layer, _):
                li = layer // 2
                pe.wait_ge(ktl_done[s], ktl_done.at(j, li + 1))
                pe.wait_ge(vl_done[s], vl_done.at(j, 2 * li + 2))
                for nt in range(CT):
                    for mt in range(CT):
                        for a, b in hi_lo:
                            mm = pe.matmul(bank[s][nt][:], KT[s][a][:, mt, nt * P:(nt + 1) * P], vv[s][b][:, mt, :],
                                           start=(mt == 0 and (a, b) == (0, 0)), stop=(mt == CT - 1 and (a, b) == (1, 0)))
                    mm.then_inc(y_ps[s], 1)

            def support(s, j, *_):
                pe.wait_ge(hl_done[s], hl_done.at(j, 4))
                for mt in range(CT):
                    for nt in range(CT):
                        for a, b in hi_lo:
                            mm = pe.matmul(bank[s][mt][:], adj2[a][:, nt, mt * P:(mt + 1) * P], h[s][b][:, nt, :],
                                           start=(nt == 0 and (a, b) == (0, 0)), stop=(nt == CT - 1 and (a, b) == (1, 0)))
                    mm.then_inc(y_ps[s], 1)

            run(pe, {"P1": p1, "P2": p2, "P3": p3, "P4a": p4a, "P4b": p4b, "T": transposes,
                     "Zl": project("lang"), "Zg": project("grav"), "Gl": gram("lang"), "Gg": gram("grav"),
                     "Rl": rows("lang"), "Rg": rows("grav"), "V": values, "KT": mixture_t, "Y": apply,
                     "Y2": support})

        @block.scalar
        def _(act):
            def h_hi(s, j, layer, _):
                if layer in (0, 2):
                    for ct in range(CT):
                        act.wait_ge(t_done[s], t_done.at(j, 2 * layer + ct + 1))
                        act.activation(h[s][0][:, ct, :], t_ln[s][:, ct, :], ACT.Relu).then_inc(hh_done[s], 1)

            def p1(s, j, *_):
                for b in range(2):
                    act.wait_ge(pt_done[s], pt_done.at(j, b + 1))
                    act.activation(PT[s][0][:, 2 * b:2 * b + 2, :], bank[s][b][:], ACT.Copy, scale=PT_SCALE / H_SCALE).then_inc(pth_done[s], 1)
                    if b == 0:
                        continue
                    act.wait_ge(qk_done[s], qk_done.at(j, 1))
                    act.activation(qk[s][:], bank[s][2][:, 0:2 * NT], ACT.Copy, scale=qk_unscale[:]).then_inc(qkc_done[s], 1)

            def p2(s, j, *_):
                act.wait_ge(Q_done[s], Q_done.at(j, 1))
                act.activation(ea[s][:], qd[s][:], ACT.Exp)
                act.activation(eb[s][:], qd[s][:], ACT.Exp, scale=SLOPE)
                act.activation(r12[s][:, 0, :], bank[s][3][:], ACT.Relu, scale=-1.0, bias=nQ[s][:])
                act_chain.link(act, act.activation(r12[s][:, 1, :], bank[s][3][:], ACT.Relu, bias=Q[s][:]), s, j)
                act.activation(uv[s][:], r12[s][:], ACT.Exp, scale=SLOPE - 1.0).then_inc(uv_done[s], 1)
                for nt in range(NT):
                    act.wait_ge(e_done[s], e_done.at(j, nt + 1))
                    act.activation(E16[s][0][:, nt, :], E[s][:, nt, :], ACT.Copy, scale=E_SCALE).then_inc(eh_done[s], 1)

            def p4b(s, j, *_):
                act.wait_ge(rsr_done[s], rsr_done.at(j, 1))
                act.activation(rsx[s][:], bank[s][3][:], ACT.Copy).then_inc(rsx_done[s], 1)
                for ot in range(CT):
                    act.wait_ge(om_done[s], om_done.at(j, ot + 1))
                    act.activation(orl[s][:, ot, :], orl[s][:, ot, :], ACT.Relu, scale=l0_unscale[:], bias=bm_col[:, ot:ot + 1]).then_inc(orl_done[s], 1)

            def transposes(s, j, layer, _):
                li = layer // 2
                for b in range(2):
                    act.wait_ge(hT_ps[s], hT_ps.at(j, 2 * li + b + 1))
                    act.activation(hT[s][0][:, 2 * b:2 * b + 2, :], bank[s][b][:], ACT.Relu).then_inc(hTh_done[s], 1)

            def project(which):
                def stage(s, j, layer, half):
                    li = layer // 2
                    z, b0, k = (zl, 2, 0) if which == "lang" else (zg, 0, 2)
                    act.wait_ge(z_ps[s], z_ps.at(j, 4 * li + k + half + 1))
                    act.activation(z[s][0][:, 2 * half:2 * half + 2, :], bank[s][b0 + half][:], ACT.Copy, scale=1.0 / H_SCALE).then_inc(zh_done[s], 1)
                return stage

            def rows_l(s, j, layer, _):
                li = layer // 2
                act.wait_ge(rsl_done[s], rsl_done.at(j, li + 1))
                act.wait_ge(gl_ps[s], gl_ps.at(j, li + 1))
                for nt in range(CT):
                    a = act.activation(tl[s][:, nt, :], bank[s][2][:, nt * C:(nt + 1) * C], ACT.Relu,
                                       scale=rsl[s][:, nt:nt + 1])
                a.then_inc(tl_done[s], 1)

            def rows_g(s, j, layer, _):
                li = layer // 2
                act.wait_ge(rg_ps[s], rg_ps.at(j, li + 1))
                act.activation(sqr[s][:], bank[s][0][:, C:2 * C], ACT.Copy, scale=-0.5).then_inc(sqr_done[s], 1)
                act.wait_ge(e0_done[s], e0_done.at(j, li + 1))
                act.wait_ge(bg_done[s], bg_done.at(j, li + 1))
                for nt in range(CT):
                    a = act.activation(Eg[s][:, nt, :], e0[s][:, nt, :], ACT.Exp, scale=two_c[:, li:li + 1],
                                       bias=bg[s][:, nt:nt + 1])
                a.then_inc(eg_done[s], 1)
                act.wait_ge(rdeg_done[s], rdeg_done.at(j, li + 1))
                for nt in range(CT):
                    a = act.activation(Eg[s][:, nt, :], Bg[s][:, nt, :], ACT.Copy, scale=rdeg[s][:, 1, nt:nt + 1])
                a.then_inc(kg_done[s], 1)

            def values(s, j, layer, half):
                li = layer // 2
                act.wait_ge(v_ps[s], v_ps.at(j, 2 * li + half + 1))
                act.activation(vv[s][0][:, half, :], bank[s][1 + half][:], ACT.Copy, scale=1.0 / H_SCALE).then_inc(vh_done[s], 1)

            def mixture_t(s, j, layer, _):
                li = layer // 2
                act.wait_ge(kt_ps[s], kt_ps.at(j, li + 1))
                act.activation(KT[s][0][:], bank[s][3][:], ACT.Copy).then_inc(kth_done[s], 1)

            def apply(s, j, layer, _):
                if layer == 3:
                    act.wait_ge(x4_done[s], x4_done.at(j, 2))
                    act.dma_start(out_dram[2 * j + s], xs[s][:]).then_inc(x_stored[s], 16)
                    act_chain.end_sample(s)

            run(act, {"N": h_hi, "P1": p1, "P2": p2, "P4b": p4b, "T": transposes, "Zl": project("lang"),
                      "Zg": project("grav"), "Rl": rows_l, "Rg": rows_g, "V": values, "KT": mixture_t, "Y": apply})
            for s in range(2):
                if later(PAIRS):
                    act.wait_ge(x_stored[s], x_stored.at(PAIRS, 0))

        @block.vector
        def _(dve):
            def norm(s, j, layer, _):
                src = xin[s] if layer == 0 else xs[s]
                if layer == 0:
                    dve.wait_ge(xin_landed[s], xin_landed.at(j, 1))
                for ct in range(CT):
                    a = dve.bn_stats(stats[s][:, ct, :], src[:, ct, :])
                dve_chain.link(dve, a, s, j)
                dve.tensor_copy(carry[s][:], stats[s][:, 0, 0:1])
                for ct in range(CT):
                    a = dve.bn_aggr(mv[s][:, ct, :], stats[s][:, ct, :])
                dve_chain.link(dve, a, s, j)
                dve.tensor_scalar(var_in[s][:], mv[s][:, :, 1], LN_EPS, 1.0 / (H_SCALE * H_SCALE),
                                  ALU.add, ALU.mult).then_inc(stats_done[s], 1)
                dve.wait_ge(rstd_done[s], rstd_done.at(j, layer + 1))
                for ct in range(CT):
                    dve.tensor_scalar(t_ln[s][:, ct, :], src[:, ct, :], mv[s][:, ct, 0:1], rstd[s][:, ct:ct + 1], ALU.subtract, ALU.mult).then_inc(t_done[s], 1)
                if layer in (0, 2):
                    for ct in range(CT):
                        dve.wait_ge(hh_done[s], hh_done.at(j, layer + ct + 1))
                        dve.scalar_tensor_tensor(h[s][1][:, ct, :], t_ln[s][:, ct, :], 0.0, h[s][0][:, ct, :], ALU.max, ALU.subtract).then_inc(hl_done[s], 1)

            def p1(s, j, *_):
                for b in range(2):
                    dve.wait_ge(pth_done[s], pth_done.at(j, b + 1))
                    dve.scalar_tensor_tensor(PT[s][1][:, 2 * b:2 * b + 2, :], bank[s][b][:], PT_SCALE / H_SCALE, PT[s][0][:, 2 * b:2 * b + 2, :], ALU.mult, ALU.subtract).then_inc(ptl_done[s], 1)
                dve.wait_ge(qkc_done[s], qkc_done.at(j, 1))
                dve.tensor_reduce(qm[s][:], qk[s][:, :, 0], AX_X, ALU.max).then_inc(qm_done[s], 1)

            def p2(s, j, *_):
                dve.wait_ge(qmr_done[s], qmr_done.at(j, 1))
                dve_chain.link(dve, dve.tensor_reduce(Q[s][:], bank[s][2][:, P:2 * P], AX_X, ALU.max), s, j)
                dve.tensor_scalar(nQ[s][:], Q[s][:], -1.0, None, ALU.mult)
                dve.tensor_scalar(qd[s][:], qk[s][:, :, 0], Q[s][:], None, ALU.subtract).then_inc(Q_done[s], 1)
                dve.wait_ge(uv_done[s], uv_done.at(j, 1))
                for nt in range(NT + 1):
                    if nt < NT:
                        a = dve.tensor_scalar(tmp[:, nt % 2, :], uv[s][:, 1, :], eb[s][:, nt:nt + 1], None, ALU.mult)
                        dve_chain.link(dve, a, s, j)
                        dve.scalar_tensor_tensor(E[s][:, nt, :], uv[s][:, 0, :], ea[s][:, nt:nt + 1], tmp[:, nt % 2, :], ALU.mult, ALU.max).then_inc(e_done[s], 1)
                    if nt > 0:
                        dve.wait_ge(eh_done[s], eh_done.at(j, nt))
                        dve.scalar_tensor_tensor(E16[s][1][:, nt - 1, :], E[s][:, nt - 1, :], E_SCALE, E16[s][0][:, nt - 1, :], ALU.mult, ALU.subtract).then_inc(el_done[s], 1)

            def p4a(s, j, *_):
                dve.wait_ge(scol_done[s], scol_done.at(j, 1))
                dve.reciprocal(rs0[s][:], bank[s][2][:, 0:NT]).then_inc(rs0_done[s], 1)

            def p4b(s, j, *_):
                dve.wait_ge(rsx_done[s], rsx_done.at(j, 1))
                dve.wait_ge(out_done[s], out_done.at(j, 1))
                for ot in range(CT):
                    dve.tensor_tensor(orl[s][:, ot, :], bank[s][ot][:], rsx[s][:], ALU.mult).then_inc(om_done[s], 1)
                if later(j):
                    dve.wait_ge(x_stored[s], x_stored.at(j, 0))
                for ot in range(CT):
                    dve.wait_ge(orl_done[s], orl_done.at(j, ot + 1))
                    a = dve.tensor_tensor(xs[s][:, ot, :], orl[s][:, ot, :], xin[s][:, ot, :], ALU.add)
                    a.then_inc(x1_done[s], 1)
                dve.wait_ge(x1_done[s], x1_done.at(j, 2))

            def transposes(s, j, layer, _):
                li = layer // 2
                for b in range(2):
                    dve.wait_ge(hTh_done[s], hTh_done.at(j, 2 * li + b + 1))
                    dve.scalar_tensor_tensor(hT[s][1][:, 2 * b:2 * b + 2, :], bank[s][b][:], 0.0, hT[s][0][:, 2 * b:2 * b + 2, :], ALU.max, ALU.subtract).then_inc(hTl_done[s], 1)

            def project(which):
                def stage(s, j, layer, half):
                    li = layer // 2
                    z, b0, k = (zl, 2, 0) if which == "lang" else (zg, 0, 2)
                    dve.wait_ge(zh_done[s], zh_done.at(j, 4 * li + k + half + 1))
                    dve.scalar_tensor_tensor(z[s][1][:, 2 * half:2 * half + 2, :], bank[s][b0 + half][:], 1.0 / H_SCALE, z[s][0][:, 2 * half:2 * half + 2, :], ALU.mult, ALU.subtract).then_inc(zlo_done[s], 1)
                return stage

            def diagonal(which):
                def stage(s, j, layer, _):
                    li = layer // 2
                    ps, b0, d, done = ((gl_ps, 2, dgl, dgl_done) if which == "lang" else (gg_ps, 3, dgg, dgg_done))
                    dve.wait_ge(ps[s], ps.at(j, li + 1))
                    for nt in range(CT):
                        a = dve.scalar_tensor_tensor(diag[s][:, int(which == "grav"), nt, :], bank[s][b0][:, nt * (C + P):nt * (C + P) + P], 1.0,
                                                     ident[:], ALU.mult, ALU.mult, accum_out=d[s][:, nt:nt + 1])
                    if which == "lang":
                        dve_chain.link(dve, a, s, j)
                        a = dve.tensor_scalar(nrm[s][:], dgl[s][:], norm_floor[:, li:li + 1], None, ALU.max)
                    a.then_inc(done[s], 1)
                    if which == "grav":
                        dve.wait_ge(dgg_done[s], dgg_done.at(j, li + 1))
                        dve.tensor_scalar(bg[s][:], dgg[s][:], neg_c[:, li:li + 1], None, ALU.mult).then_inc(bg_done[s], 1)
                return stage

            def rows_l(s, j, layer, _):
                li = layer // 2
                dve.wait_ge(tl_done[s], tl_done.at(j, li + 1))
                dve.wait_ge(rl_ps[s], rl_ps.at(j, li + 1))
                row = bank[s][0][:, 0:C].unsqueeze(1).to_broadcast((P, CT, C))
                dve.tensor_tensor(tl[s][:], tl[s][:], row, ALU.mult).then_inc(row_used[s], 1)
                dve.wait_ge(row_used[s], row_used.at(j, li + 1))
                for nt in range(CT):
                    a = dve.scalar_tensor_tensor(Bl[s][:, nt, :], tl[s][:, nt, :], 1.0, adj_off[:, nt, :],
                                                 ALU.mult, ALU.mult, accum_out=deg[s][:, 0, nt:nt + 1])
                dve_chain.link(dve, a, s, j)

            def rows_g(s, j, layer, _):
                li = layer // 2
                dve.wait_ge(sqr_done[s], sqr_done.at(j, li + 1))
                dve.tensor_tensor(e0[s][:], bank[s][3][:].rearrange("p (t c) -> p t c", t=CT), sqr[s][:].unsqueeze(1).to_broadcast((P, CT, C)), ALU.add).then_inc(e0_done[s], 1)
                dve.wait_ge(eg_done[s], eg_done.at(j, li + 1))
                for nt in range(CT):
                    a = dve.scalar_tensor_tensor(Bg[s][:, nt, :], Eg[s][:, nt, :], 1.0, adj_off[:, nt, :],
                                                 ALU.min, ALU.mult, accum_out=deg[s][:, 1, nt:nt + 1])
                dve_chain.link(dve, a, s, j)
                dve_chain.link(dve, dve.tensor_scalar(rdeg[s][:], deg[s][:], EPS, None, ALU.max), s, j)
                dve_chain.link(dve, dve.reciprocal(rdeg[s][:], rdeg[s][:]), s, j)
                dve.tensor_tensor(rdeg[s][:], rdeg[s][:], gates[:, li, :].unsqueeze(2).to_broadcast((P, 2, CT)), ALU.mult).then_inc(rdeg_done[s], 1)
                dve.wait_ge(rdeg_done[s], rdeg_done.at(j, li + 1))
                dve.wait_ge(kg_done[s], kg_done.at(j, li + 1))
                for nt in range(CT):
                    a = dve.scalar_tensor_tensor(Km[s][:, nt, :], Bl[s][:, nt, :], rdeg[s][:, 0, nt:nt + 1],
                                                 Eg[s][:, nt, :], ALU.mult, ALU.add)
                a.then_inc(K_done[s], 1)

            def values(s, j, layer, half):
                li = layer // 2
                dve.wait_ge(vh_done[s], vh_done.at(j, 2 * li + half + 1))
                dve.scalar_tensor_tensor(vv[s][1][:, half, :], bank[s][1 + half][:], 1.0 / H_SCALE, vv[s][0][:, half, :], ALU.mult, ALU.subtract).then_inc(vl_done[s], 1)

            def mixture_t(s, j, layer, _):
                li = layer // 2
                dve.wait_ge(kth_done[s], kth_done.at(j, li + 1))
                dve.tensor_tensor(KT[s][1][:], bank[s][3][:].rearrange("p (t c) -> p t c", t=CT), KT[s][0][:], ALU.subtract).then_inc(ktl_done[s], 1)

            def apply(s, j, layer, _):
                li = layer // 2
                done = x2_done if layer == 1 else x4_done
                for nt in range(CT):
                    dve.wait_ge(y_ps[s], y_ps.at(j, (0 if layer == 1 else 4) + nt + 1))
                    dve.scalar_tensor_tensor(xs[s][:, nt, :], bank[s][nt][:], v_unscale[:, li:li + 1], xs[s][:, nt, :], ALU.mult, ALU.add).then_inc(done[s], 1)
                if layer == 1:
                    dve.wait_ge(x2_done[s], x2_done.at(j, 2))
                if layer == 3:
                    dve_chain.end_sample(s)

            def support(s, j, *_):
                for mt in range(CT):
                    dve.wait_ge(y_ps[s], y_ps.at(j, 2 + mt + 1))
                    dve.wait_ge(xb_done[s], xb_done.at(j, mt + 1))
                    a = dve.scalar_tensor_tensor(xs[s][:, mt, :], bank[s][mt][:], l2_unscale[:], xb[s][:, mt, :],
                                                 ALU.mult, ALU.add)
                dve_chain.link(dve, a, s, j)

            run(dve, {"N": norm, "P1": p1, "P2": p2, "P4a": p4a, "P4b": p4b, "T": transposes,
                      "Zl": project("lang"), "Zg": project("grav"), "Gl": diagonal("lang"), "Gg": diagonal("grav"),
                      "Rl": rows_l, "Rg": rows_g, "V": values, "KT": mixture_t, "Y": apply, "Y2": support})

        @block.gpsimd
        def _(pool):
            def norm(s, j, layer, _):
                pool.wait_ge(stats_done[s], stats_done.at(j, layer + 1))
                pool.tensor_tensor(rstd[s][:], var_in[s][:], minus_half[:], ALU.pow).then_inc(rstd_done[s], 1)
                if layer == 2:
                    for ct in range(CT):
                        pool.tensor_tensor(xb[s][:, ct, :], xs[s][:, ct, :], bias_row[:], ALU.add).then_inc(xb_done[s], 1)

            def p2(s, j, *_):
                for k in (0, 1):
                    pool.wait_ge(e_done[s], e_done.at(j, 2 * k + 2))
                    a = pool.tensor_tensor(esum[s][:, k, :], E[s][:, 2 * k, :], E[s][:, 2 * k + 1, :], ALU.add)
                pool_chain.link(pool, a, s, j)
                pool.tensor_tensor(esum[s][:, 0, :], esum[s][:, 0, :], esum[s][:, 1, :], ALU.add).then_inc(esum_done[s], 1)

            def norms(s, j, layer, _):
                li = layer // 2
                pool.wait_ge(dgl_done[s], dgl_done.at(j, li + 1))
                pool.tensor_tensor(rsl[s][:], nrm[s][:], minus_half[:], ALU.pow).then_inc(rsl_done[s], 1)
                if layer == 3:
                    pool_chain.end_sample(s)

            run(pool, {"N": norm, "P2": p2, "Gl": norms})


_INS = ["x", "adj", "L0_gnn_wq", "L0_gnn_wk", "L0_gnn_bm",
        "L1_gnn_W_lang", "L1_gnn_W_grav", "L1_gnn_W_V", "L1_gnn_W_O", "L1_gnn_gate_logit", "L1_gnn_log_sigma",
        "L2_gnn_bias",
        "L3_gnn_W_lang", "L3_gnn_W_grav", "L3_gnn_W_V", "L3_gnn_W_O", "L3_gnn_gate_logit", "L3_gnn_log_sigma"]


def kernel(**inputs):
    import numpy as _np
    import concourse.bacc as _bacc
    from concourse import mybir as _mybir
    from concourse.bass_utils import run_bass_kernel_spmd as _run

    nc = _bacc.Bacc("TRN2", target_bir_lowering=False, num_devices=1)
    arrays, args = {}, []
    for name in _INS:
        a = _np.ascontiguousarray(inputs[name])
        if a.ndim == 0 or a.size == 1:
            a = a.reshape(1, 1)
        arrays[f"in_{name}"] = a
        args.append(nc.dram_tensor(f"in_{name}", a.shape, _mybir.dt.from_np(a.dtype), kind="ExternalInput").ap())
    shape = inputs["x"].shape
    out = nc.dram_tensor("out_0", shape, _mybir.dt.float32, kind="ExternalOutput").ap()
    build(nc, *args, out)
    r = _run(nc, [arrays], core_ids=[0])
    return r.results[0]["out_0"]
```

```python
from contextlib import ExitStack

import concourse.bass as bass
from concourse import mybir

F32 = mybir.dt.float32
F16 = mybir.dt.float16
U32 = mybir.dt.uint32
ALU = mybir.AluOpType
ACT = mybir.ActivationFunctionType
AX_X = mybir.AxisListType.X

P = 128
DVE_STEPS, ACT_STEPS, POOL_STEPS = 27, 1, 1
LN_EPS = 1e-5
EPS = 1e-8
SLOPE = 0.01

H_SCALE = 256.0
W_TOP = 8.0
PT_SCALE = 0.5
E_SCALE = 16384.0
K_SCALE = 1024.0

ORDER = {
    "pe": """
        W0AD W0MR A0AH W1MR W0TU W1TU A0QK W2TU W3PR0 W3PR1 b3L0 b3L1 W3PR2 b3GG W3PR3 b3GL A0AT0 b3RG W2MR
        A0AT1 b3RL A0AT2 A0AT3 W3MR A0SM W4TU W5TU A0SR b3V0 W6TU b3V1 W7PR0 W7PR1 b3V2 W7PR2 b3V3 W7PR3 b3KT
        A1T W4MR b3Y A1G0 A1G1 B0AH A1L0 B0QK A1L1 A1GG A1GL A1RG B0AT0 B0AT1 A1RL B0AT2 B0AT3 B0SM B0SR A1V0
        A1V1 A1KT A1V2 A1V3 B1T A1Y B1G0 B1G1 B1L0 A2S B1L1 B1GG B1GL B1RG B1V0 B1RL B1V1 B1V2 A3T B1V3 B1KT
        B1Y A3G0 A3G1 A3L0 A3L1 B2S A3GG A3GL A3RG A3V0 A3RL A3V1 A3V2 B3T A3V3 A3KT A3Y B3G0 B3G1""",
    "act": """
        W0EX W0AD A0H0 A0H1 A0AH0 A0QK W0HI W1HI A0AH1 W2CO A0UV b3G1 A0EV0 b3L0 A0EV1 b3L1 A0EH0 A0EV2 b3CG
        A0EH1 A0EV3 A0EH2 b3CL b3SQ A0EH3 W3CO W3HI b3RL W4HI b3EG W5HI b3KL A0SR W6CO A0AT0 A0AT1 W7CO b3V0
        b3V1 b3KT A1T0 A1T1 b3ST W7HI B0H0 B0H1 A1G0 A1G1 B0QK B0AH0 B0AH1 A1L0 B0UV A1L1 B0EV0 A1CG B0EV1
        B0EH0 B0EV2 B0EH1 B0EV3 A1CL A1SQ B0EH2 B0EH3 A1RL A1EG A1KL B0SR B0AT0 B0AT1 A1V0 A1KT A1V1 B1T0 B1T1
        B1G0 A2H0 A2H1 B1G1 B1L0 B1L1 B1CG B1CL B1SQ B1RL B1EG B1KL B1V0 B1V1 B1KT A3T0 A3T1 B2H0 A3G0 B2H1
        A3G1 A3L0 A3L1 A3CG A3CL A3SQ A3RL A3EG A3KL A3V0 B3T0 B3T1 A3V1 A3KT A3ST B3G0""",
    "dve": """
        W0MX A0ST W0SC A0N W0SQ W0AD A0H0 A0H1 W1MX A0AH0 W1SC A0QM W0LO W1LO A0Q b3G0 A0AH1 b3G1 A0E0 b3L0
        b3L1 A0E1 b3DG A0E2 b3DL A0E3 W2MX A0E4 W2SC W1FA b3RG W3MX b3RL W3LO W3SC A0SM W4LO W5LO b3BG A0AT0
        A0AT1 b3K A0X0 A0X1 A1ST b3V0 A1N b3V1 b3KT W4MX A1T0 A1T1 b3Y0 W4SC W3FA b3Y1 W7LO B0ST B0N B0H0 B0H1
        B0QM A1G0 B0AH0 B0Q A1G1 B0AH1 A1L0 A1L1 B0E0 A1DG B0E1 B0E2 A1DL B0E3 A1RG B0E4 A1RL B0SM A1BG B0AT0
        B0AT1 A1K B0X0 B0X1 B1ST A1V0 B1N A1V1 A1KT B1T0 B1T1 A1Y0 A1Y1 A2ST A2N A2H0 B1G0 B1G1 A2H1 B1L0 A2S0
        A2S1 A3ST B1L1 B1DG B1DL B1RG A3N B1RL B1BG B1K B1V0 B1V1 B1KT A3T0 A3T1 B1Y0 B1Y1 B2ST B2N B2H0 A3G0
        A3G1 B2H1 A3L0 B2S0 A3L1 B2S1 B3ST A3DG A3DL A3RG B3N A3RL A3BG A3K A3V0 A3V1 A3KT B3T0 B3T1 A3Y0 A3Y1""",
    "pool": """
        W0CO A0ST A0SE0 b3DL A0SE1 W0OF A1ST B0ST B0SE0 A1DL B0SE1 B1ST A2ST A2XB0 A2XB1 B1DL A3ST B2ST B2XB0
        B2XB1 B3ST A3DL""",
    "load": """
        W0C A0X W0M W1M W2M W3M B0X W4M W5M W6M W7M""",
}

class Signal:

    def __init__(self, ctx, nc, name, per, unit=1):
        self.sems = [ctx.enter_context(nc.semaphore(f"{name}_{'ab'[s]}")) for s in range(2)]
        self.per, self.unit = per, unit

    def __getitem__(self, slot):
        return self.sems[slot]

    def at(self, sample, n):
        return sample * (self.per * self.unit) + n * self.unit


class Chain(Signal):

    def __init__(self, ctx, nc, name, per):
        super().__init__(ctx, nc, name, per)
        self.n = [0, 0]

    def link(self, eng, ins, slot, sample):
        self.n[slot] += 1
        ins.then_inc(self[slot], 1)
        eng.wait_ge(self[slot], self.at(sample, self.n[slot]))

    def end_sample(self, slot):
        assert self.n[slot] == self.per, (self.n[slot], self.per)
        self.n[slot] = 0


def later(sample):
    return not isinstance(sample, int) or sample > 0


def build(nc, x, adj, wq, wk, bm, w_lang1, w_grav1, w_v1, w_o1, gate1, sigma1, bias2,
          w_lang3, w_grav3, w_v3, w_o3, gate3, sigma3, out):
    B, C, N = x.shape
    CT, NT, DT = C // P, N // P, N // P
    PAIRS = B // 2
    x_dram = x.rearrange("b (t p) n -> b p t n", p=P)
    out_dram = out.rearrange("b (t p) n -> b p t n", p=P)

    with ExitStack() as ctx:
        def sb(name, shape, dt=F32):
            return ctx.enter_context(nc.sbuf_tensor(name, shape, dt))

        def one(name):
            return ctx.enter_context(nc.semaphore(name))

        def signal(name, per, unit=1):
            return Signal(ctx, nc, name, per, unit)

        ident = sb("ident", [P, P])
        ones = sb("ones", [P, 1])
        minus_half = sb("minus_half", [P, CT])
        adj_sb = sb("adj_sb", [P, CT, C])
        adj_off = sb("adj_off", [P, CT, C])
        adjT = [sb(f"adjT_{p}", [P, CT, C], F16) for p in "hl"]
        adj2 = [sb(f"adj2_{p}", [P, CT, C], F16) for p in "hl"]
        wqk_f = sb("wqk_f", [P, CT, 2])
        wqk = [sb(f"wqk_{p}", [P, CT, 2], F16) for p in "hl"]
        bm_col = sb("bm_col", [P, CT])
        bias_row = sb("bias_row", [P, N])
        weight = {}
        for layer in (1, 3):
            for name in ("lang", "grav", "vo"):
                weight[name, layer] = [sb(f"w_{name}{layer}_{p}", [P, DT, N], F16) for p in "hl"]
        MATS = ["adj", "qk", "lang1", "grav1", "vo1", "lang3", "grav3", "vo3"]
        SCALE_SETS = [["adj", "qk"], ["lang1", "grav1"], ["vo1"], ["lang3", "grav3"], ["vo3"]]
        scale = sb("scale", [P, len(MATS), 1])
        inv = sb("inv", [P, len(MATS), 1])
        part_max = sb("part_max", [P, len(MATS), 2])
        abs_max = sb("abs_max", [P, len(MATS)])
        scratch = sb("scratch", [P, 3, 2])

        def s_of(name):
            return scale[:, MATS.index(name), :]

        def i_of(name):
            return inv[:, MATS.index(name), :]

        qk_unscale = sb("qk_unscale", [P, 1])
        l0_unscale = sb("l0_unscale", [P, 1])
        l2_unscale = sb("l2_unscale", [P, 1])
        gates = sb("gates", [P, 2, 2])
        norm_floor = sb("norm_floor", [P, 2])
        two_c = sb("two_c", [P, 2])
        neg_c = sb("neg_c", [P, 2])
        v_unscale = sb("v_unscale", [P, 2])
        gl = sb("gl", [P, 4])
        small = sb("small", [P, 8])

        def both(name, shape, dt=F32):
            return [sb(f"{name}_{c}", shape, dt) for c in "ab"]

        def both2(name, shape):
            return [[sb(f"{name}{p}_{c}", shape, F16) for p in "hl"] for c in "ab"]

        xin = both("xin", [P, CT, N])
        xs = both("xs", [P, CT, N])
        t_ln = both("t_ln", [P, CT, N])
        xb = both("xb", [P, CT, N])
        stats = both("stats", [P, CT, 6])
        mv = both("mv", [P, CT, 2])
        var_in = both("var_in", [P, CT])
        rstd = both("rstd", [P, CT])
        h = both2("h", [P, CT, N])
        PT = both2("PT", [P, NT, C])
        qk = both("qk", [P, NT, 2])
        qm = both("qm", [P, 1])
        Q = both("Q", [P, 1])
        nQ = both("nQ", [P, 1])
        qd = both("qd", [P, NT])
        ea = both("ea", [P, NT])
        eb = both("eb", [P, NT])
        r12 = both("r12", [P, 2, N])
        uv = both("uv", [P, 2, N])
        tmp = both("tmp", [P, 2, N])
        E = both("E", [P, NT, N])
        E16 = both2("E", [P, NT, N])
        esum = both("esum", [P, 2, N])
        rs0 = both("rs0", [P, NT])
        rsx = both("rsx", [P, N])
        orl = r12
        hT = both2("hT", [P, DT, C])
        zl = both2("zl", [P, DT, C])
        zg = both2("zg", [P, DT, C])
        vv = [[e[:, 0:CT, :] for e in E16[s]] for s in range(2)]
        KT = [[e[:, CT, :].rearrange("p (t c) -> p t c", t=CT) for e in E16[s]] for s in range(2)]

        def tile_of(buf, n):
            return [buf[s][:, n, :].rearrange("p (t c) -> p t c", t=CT) for s in range(2)]

        diag = both("diag", [P, 2, CT, P])
        carry = both("carry", [P, 1])
        dgl = both("dgl", [P, CT])
        dgg = both("dgg", [P, CT])
        nrm = both("nrm", [P, CT])
        rsl = both("rsl", [P, CT])
        bg = both("bg", [P, CT])
        sqr = both("sqr", [P, C])
        g01 = [uv[s][:, 0, 0:2 * P].rearrange("p (k m) -> p k m", k=2) for s in range(2)]
        tl = tile_of(E, 0)
        Bl = tile_of(E, 1)
        e0 = tile_of(E, 2)
        Eg = tile_of(E, 3)
        Bg = tile_of(xb, 0)
        deg = both("deg", [P, 2, CT])
        rdeg = both("rdeg", [P, 2, CT])
        Km = tile_of(xb, 1)
        bank = [[ctx.enter_context(nc.psum_tensor(f"bank{b}_{c}", [P, 512], F32)) for b in range(4)]
                for c in "ab"]

        xin_landed = signal("xin_landed", 1, 16)
        x_stored = signal("x_stored", 1, 16)
        x1_done = signal("x1_done", 2)
        x2_done = signal("x2_done", 2)
        x4_done = signal("x4_done", 2)
        xb_done = signal("xb_done", 2)
        stats_done = signal("stats_done", 4)
        rstd_done = signal("rstd_done", 4)
        t_done = signal("t_done", 8)
        hh_done = signal("hh_done", 4)
        hl_done = signal("hl_done", 4)
        pt_done = signal("pt_done", 2)
        pth_done = signal("pth_done", 2)
        ptl_done = signal("ptl_done", 2)
        qk_done = signal("qk_done", 1)
        qkc_done = signal("qkc_done", 1)
        qm_done = signal("qm_done", 1)
        qmr_done = signal("qmr_done", 1)
        Q_done = signal("Q_done", 1)
        uv_done = signal("uv_done", 1)
        ev_done = signal("ev_done", 4)
        e_done = signal("e_done", 4)
        eh_done = signal("eh_done", 4)
        el_done = signal("el_done", 4)
        esum_done = signal("esum_done", 1)
        out_done = signal("out_done", 1)
        scol_done = signal("scol_done", 1)
        rs0_done = signal("rs0_done", 1)
        rsr_done = signal("rsr_done", 1)
        rsx_done = signal("rsx_done", 1)
        om_done = signal("om_done", 2)
        orl_done = signal("orl_done", 2)
        hT_ps = signal("hT_ps", 4)
        hTh_done = signal("hTh_done", 4)
        hTl_done = signal("hTl_done", 4)
        z_ps = signal("z_ps", 8)
        zh_done = signal("zh_done", 8)
        zlo_done = signal("zlo_done", 8)
        gl_ps = signal("gl_ps", 2)
        gg_ps = signal("gg_ps", 2)
        dgl_done = signal("dgl_done", 2)
        dgg_done = signal("dgg_done", 2)
        g01_done = signal("g01_done", 4)
        rsl_done = signal("rsl_done", 2)
        bg_done = signal("bg_done", 2)
        rl_ps = signal("rl_ps", 2)
        row_used = signal("row_used", 2)
        rg_ps = signal("rg_ps", 2)
        sqr_done = signal("sqr_done", 2)
        tl_done = signal("tl_done", 2)
        e0_done = signal("e0_done", 2)
        eg_done = signal("eg_done", 2)
        rdl_done = signal("rdl_done", 2)
        kl_done = signal("kl_done", 2)
        K_done = signal("K_done", 2)
        v_ps = signal("v_ps", 4)
        vh_done = signal("vh_done", 4)
        vl_done = signal("vl_done", 4)
        kt_ps = signal("kt_ps", 2)
        kth_done = signal("kth_done", 2)
        ktl_done = signal("ktl_done", 2)
        y_ps = signal("y_ps", 6)
        dve_chain = Chain(ctx, nc, "dve_chain", DVE_STEPS)
        act_chain = Chain(ctx, nc, "act_chain", ACT_STEPS)
        pool_chain = Chain(ctx, nc, "pool_chain", POOL_STEPS)

        staging = [[E[1][:, 0:2, :], E[1][:, 2:4, :]], [t_ln[1][:], xb[1][:]], [r12[1][:], uv[1][:]],
                   [tmp[1][:], esum[1][:]]]
        wo_t = [xs[1], xb[0]]
        product_f = staging[2]
        LOADS = 16 * 9
        w_landed = [one(f"w_landed_{k}") for k in range(4)]
        c_landed = one("c_landed")
        consts_made = one("consts_made")
        max_found = one("max_found")
        max_row = one("max_row")
        scaled = one("scaled")
        adj_turned = one("adj_turned")
        adj_hi = one("adj_hi")
        squared = one("squared")
        tile_ps = one("tile_ps")
        copied = one("copied")
        w_hi = one("w_hi")
        w_lo = one("w_lo")
        prep_exp = one("prep_exp")
        prep_chain = one("prep_chain")
        JOBS = []
        for layer, wl, wg, wo, wv in ((1, w_lang1, w_grav1, w_o1, w_v1), (3, w_lang3, w_grav3, w_o3, w_v3)):
            JOBS += [(wl, "turn", f"lang{layer}"), (wg, "turn", f"grav{layer}"), (wo, "keep", None),
                     (wv, "multiply", f"vo{layer}")]

        def splits(k):
            return DT * sum(how != "keep" for _, how, _ in JOBS[:k])

        def copies(k):
            return DT * sum(how != "turn" for _, how, _ in JOBS[:k])

        def set_of(name):
            return next(n for n, names in enumerate(SCALE_SETS) if name in names)

        def tile_bank(tile):
            return bank[1][tile % 3]

        def run(eng, name, steps):
            def write(i, slots):
                for step in ORDER[name].split():
                    if step[0] in slots:
                        number = int(step[-1]) if step[-1].isdigit() else 0
                        steps[step[2:].rstrip("0123456789")](int(step[0] != "A"), i - (step[0] == "b"), int(step[1]), number)

            write(0, "WAB")
            with eng.Fori(1, PAIRS) as i:
                write(i, "bAB")
            write(PAIRS, "b")

        block = ctx.enter_context(nc.Block())

        @block.sync
        def _(sp):
            def load(s, j, layer, n):
                if later(j):
                    sp.wait_ge(x1_done[s], x1_done.at(j, 0))
                sp.dma_start(xin[s][:], x_dram[2 * j + s]).then_inc(xin_landed[s], 16)

            def load_small(s, j, layer, n):
                with nc.allow_non_contiguous_dma(reason="a few small vectors"):
                    sp.dma_start(adj_sb[:], adj.rearrange("(t p) m -> p t m", p=P)).then_inc(c_landed, 16)
                    sp.dma_start(wqk_f[:, :, 0], wq.rearrange("(t p) -> p t", p=P)).then_inc(c_landed, 16)
                    sp.dma_start(wqk_f[:, :, 1], wk.rearrange("(t p) -> p t", p=P)).then_inc(c_landed, 16)
                    sp.dma_start(bm_col[:], bm.rearrange("(t p) -> p t", p=P)).then_inc(c_landed, 16)
                    sp.dma_start(bias_row[:], bias2.partition_broadcast(P)).then_inc(c_landed, 16)
                    for k, a in enumerate((gate1, gate3, sigma1, sigma3)):
                        sp.dma_start(gl[:, k:k + 1], a.to_broadcast((P, 1))).then_inc(c_landed, 16)

            def load_matrix(s, j, job, n):
                if job >= 4:
                    sp.wait_ge(w_lo, splits(min(job - 3, 4)) if job < 6 else splits(4))
                w = JOBS[job][0].rearrange("(t p) n -> p t n", p=P)
                for half in range(2):
                    sp.dma_start(staging[job % 4][half], w[:, 2 * half:2 * half + 2, :]).then_inc(w_landed[job % 4], 16)

            run(sp, "load", {"X": load, "C": load_small, "M": load_matrix})

        @block.tensor
        def _(pe):
            hi_lo = ((0, 0), (0, 1), (1, 0))

            def first_of(t, ab):
                return t == 0 and ab == hi_lo[0]

            def last_of(t, tiles, ab):
                return t == tiles - 1 and ab == hi_lo[-1]

            def adj_h(s, j, layer, n):
                if later(j):
                    pe.wait_ge(x4_done[s], x4_done.at(j, 0))
                pe.wait_ge(hl_done[s], hl_done.at(j, 2))
                for nt in range(NT):
                    o = bank[s][nt // 2][:, (nt % 2) * C:(nt % 2 + 1) * C]
                    qo = bank[s][2][:, 2 * nt:2 * nt + 2]
                    for ct in range(CT):
                        for a, b in hi_lo:
                            lhs = h[s][a][:, ct, nt * P:(nt + 1) * P]
                            start, stop = first_of(ct, (a, b)), last_of(ct, CT, (a, b))
                            mm = pe.matmul(o, lhs, adjT[b][:, ct, :], start=start, stop=stop)
                            mq = pe.matmul(qo, lhs, wqk[b][:, ct, :], start=start, stop=stop)
                    if nt % 2 == 1:
                        mm.then_inc(pt_done[s], 1)
                mq.then_inc(qk_done[s], 1)

            def q_k_rows(s, j, layer, n):
                pe.wait_ge(qm_done[s], qm_done.at(j, 1))
                pe.transpose(bank[s][2][:, P:2 * P], qm[s][:, 0:1].to_broadcast((P, P)), ident[:])
                for nt in range(NT):
                    mm = pe.transpose(bank[s][3][:, nt * P:(nt + 1) * P],
                                      qk[s][:, nt, 1:2].to_broadcast((P, P)), ident[:])
                mm.then_inc(qmr_done[s], 1)

            def attend(s, j, layer, nt):
                if nt % 2 == 0:
                    pe.wait_ge(ptl_done[s], ptl_done.at(j, nt // 2 + 1))
                pe.wait_ge(el_done[s], el_done.at(j, nt + 1))
                for ot in range(CT):
                    for a, b in hi_lo:
                        mm = pe.matmul(bank[s][ot][:], PT[s][a][:, nt, ot * P:(ot + 1) * P], E16[s][b][:, nt, :],
                                       start=first_of(nt, (a, b)), stop=last_of(nt, NT, (a, b)))
                if nt == NT - 1:
                    mm.then_inc(out_done[s], 1)

            def sums(s, j, layer, n):
                pe.wait_ge(esum_done[s], esum_done.at(j, 1))
                for mt in range(NT):
                    mm = pe.matmul(bank[s][2][:, mt:mt + 1], esum[s][:, 0, mt * P:(mt + 1) * P], ones[:],
                                   start=True, stop=True)
                mm.then_inc(scol_done[s], 1)

            def sums_row(s, j, layer, n):
                pe.wait_ge(rs0_done[s], rs0_done.at(j, 1))
                for mt in range(NT):
                    mm = pe.transpose(bank[s][3][:, mt * P:(mt + 1) * P],
                                      rs0[s][:, mt:mt + 1].to_broadcast((P, P)), ident[:])
                mm.then_inc(rsr_done[s], 1)

            def turn(s, j, layer, n):
                pe.wait_ge(t_done[s], t_done.at(j, 2 * layer + 2))
                for dt in range(DT):
                    for ct in range(CT):
                        mm = pe.transpose(bank[s][dt // 2][:, (dt % 2) * C + ct * P:(dt % 2) * C + (ct + 1) * P],
                                          t_ln[s][:, ct, dt * P:(dt + 1) * P], ident[:])
                    if dt % 2 == 1:
                        mm.then_inc(hT_ps[s], 1)

            def project(which):
                def step(s, j, layer, half):
                    if which == "grav" and half == 0:
                        pe.wait_ge(hTl_done[s], hTl_done.at(j, 2 * (layer // 2) + 2))
                    w = weight[which, layer]
                    to = bank[s][(2 if which == "grav" else 0) + half]
                    for e in (0, 1):
                        et = 2 * half + e
                        for dt in range(DT):
                            for a, b in hi_lo:
                                mm = pe.matmul(to[:, e * C:(e + 1) * C], w[a][:, dt, et * P:(et + 1) * P],
                                               hT[s][b][:, dt, :], start=first_of(dt, (a, b)),
                                               stop=last_of(dt, DT, (a, b)))
                    mm.then_inc(z_ps[s], 1)
                return step

            def gram(which):
                def step(s, j, layer, n):
                    li = layer // 2
                    z, to, k, done = ((zg, bank[s][2], 2, gg_ps) if which == "grav" else (zl, bank[s][3], 4, gl_ps))
                    pe.wait_ge(zlo_done[s], zlo_done.at(j, 4 * li + k))
                    for nt in range(CT):
                        m0 = nt * P
                        for et in range(DT):
                            for a, b in hi_lo:
                                mm = pe.matmul(to[:, nt * C + m0:(nt + 1) * C], z[s][a][:, et, nt * P:(nt + 1) * P],
                                               z[s][b][:, et, m0:C], start=first_of(et, (a, b)),
                                               stop=last_of(et, DT, (a, b)))
                    mm.then_inc(done[s], 1)
                return step

            def rows(which):
                def step(s, j, layer, n):
                    li = layer // 2
                    src, c0, k, ready, done = ((dgg, C, 0, dgg_done, rg_ps) if which == "grav"
                                               else (rsl, 0, 1, rsl_done, rl_ps))
                    pe.wait_ge(ready[s], ready.at(j, li + 1))
                    pe.wait_ge(g01_done[s], g01_done.at(j, 2 * li + k + 1))
                    pe.transpose(bank[s][2 + k][:, C:C + P], g01[s][:, k, :], ident[:])
                    if which == "lang":
                        pe.wait_ge(sqr_done[s], sqr_done.at(j, li + 1))
                    for mt in range(CT):
                        mm = pe.transpose(bank[s][0][:, c0 + mt * P:c0 + (mt + 1) * P],
                                          src[s][:, mt:mt + 1].to_broadcast((P, P)), ident[:])
                    mm.then_inc(done[s], 1)
                return step

            def values(s, j, layer, quarter):
                half, part = quarter // 2, quarter % 2
                if quarter == 0:
                    pe.wait_ge(zlo_done[s], zlo_done.at(j, 4 * (layer // 2) + 4))
                if quarter == 2:
                    pe.wait_ge(e0_done[s], e0_done.at(j, layer // 2 + 1))
                w = weight["vo", layer]
                for dt in range(part * DT // 2, (part + 1) * DT // 2):
                    for a, b in hi_lo:
                        mm = pe.matmul(bank[s][1 + half][:], hT[s][a][:, dt, half * P:(half + 1) * P], w[b][:, dt, :],
                                       start=first_of(dt, (a, b)), stop=last_of(dt, DT, (a, b)))
                if part == 1:
                    mm.then_inc(v_ps[s], 1)

            def turn_k(s, j, layer, n):
                pe.wait_ge(K_done[s], K_done.at(j, layer // 2 + 1))
                for mt in range(CT):
                    for nt in range(CT):
                        mm = pe.transpose(bank[s][3][:, mt * C + nt * P:mt * C + (nt + 1) * P],
                                          Km[s][:, nt, mt * P:(mt + 1) * P], ident[:])
                mm.then_inc(kt_ps[s], 1)

            def apply(s, j, layer, n):
                li = layer // 2
                pe.wait_ge(ktl_done[s], ktl_done.at(j, li + 1))
                pe.wait_ge(vl_done[s], vl_done.at(j, 2 * li + 2))
                for nt in range(CT):
                    for mt in range(CT):
                        for a, b in hi_lo:
                            mm = pe.matmul(bank[s][nt][:], KT[s][a][:, mt, nt * P:(nt + 1) * P], vv[s][b][:, mt, :],
                                           start=first_of(mt, (a, b)), stop=last_of(mt, CT, (a, b)))
                    mm.then_inc(y_ps[s], 1)

            def support(s, j, layer, n):
                pe.wait_ge(hl_done[s], hl_done.at(j, 4))
                for mt in range(CT):
                    for nt in range(CT):
                        for a, b in hi_lo:
                            mm = pe.matmul(bank[s][mt][:], adj2[a][:, nt, mt * P:(mt + 1) * P], h[s][b][:, nt, :],
                                           start=first_of(nt, (a, b)), stop=last_of(nt, CT, (a, b)))
                    mm.then_inc(y_ps[s], 1)

            def adj_turn(s, j, layer, n):
                pe.wait_ge(c_landed, LOADS)
                pe.wait_ge(consts_made, 4)
                for ct in range(CT):
                    for ot in range(CT):
                        mm = pe.transpose(bank[0][0][:, ct * C + ot * P:ct * C + (ot + 1) * P],
                                          adj_sb[:, ot, ct * P:(ct + 1) * P], ident[:])
                mm.then_inc(adj_turned, 1)

            def max_rows(s, j, k, n):
                pe.wait_ge(consts_made, 4)
                pe.wait_ge(max_found, k + 1)
                if k:
                    pe.wait_ge(scaled, k)
                for i, name in enumerate(SCALE_SETS[k]):
                    m = MATS.index(name)
                    mm = pe.transpose(bank[1][3][:, i * P:(i + 1) * P], abs_max[:, m:m + 1].to_broadcast((P, P)),
                                      ident[:])
                mm.then_inc(max_row, 1)

            def bank_free(tile):
                if tile >= 3:
                    k, dt = divmod(tile - 3, DT)
                    if JOBS[k][1] == "turn":
                        pe.wait_ge(w_lo, splits(k) + dt + 1)
                    else:
                        pe.wait_ge(copied, copies(k) + dt + 1)

            def matrix_turn(s, j, job, n):
                pe.wait_ge(w_landed[job % 4], 32 * (job // 4 + 1))
                for dt in range(DT):
                    bank_free(job * DT + dt)
                    for et in range(DT):
                        mm = pe.transpose(tile_bank(job * DT + dt)[:, et * P:(et + 1) * P],
                                          staging[job % 4][et // 2][:, et % 2, dt * P:(dt + 1) * P], ident[:])
                    mm.then_inc(tile_ps, 1)

            def matrix_product(s, j, job, dt):
                pe.wait_ge(w_landed[job % 4], 32 * (job // 4 + 1))
                pe.wait_ge(copied, copies(job))
                bank_free(job * DT + dt)
                for kt in range(DT):
                    mm = pe.matmul(tile_bank(job * DT + dt)[:], staging[job % 4][kt // 2][:, kt % 2, dt * P:(dt + 1) * P],
                                   wo_t[kt // 2][:, kt % 2, :], start=kt == 0, stop=kt == DT - 1)
                mm.then_inc(tile_ps, 1)

            run(pe, "pe", {"AD": adj_turn, "MR": max_rows, "TU": matrix_turn, "PR": matrix_product,
                           "AH": adj_h, "QK": q_k_rows, "AT": attend, "SM": sums, "SR": sums_row, "T": turn,
                           "L": project("lang"), "G": project("grav"), "GL": gram("lang"), "GG": gram("grav"),
                           "RL": rows("lang"), "RG": rows("grav"), "V": values, "KT": turn_k, "Y": apply,
                           "S": support})

        @block.scalar
        def _(act):
            def h_hi(s, j, layer, ct):
                act.wait_ge(t_done[s], t_done.at(j, 2 * layer + ct + 1))
                act.activation(h[s][0][:, ct, :], t_ln[s][:, ct, :], ACT.Relu).then_inc(hh_done[s], 1)

            def adj_h_hi(s, j, layer, b):
                act.wait_ge(pt_done[s], pt_done.at(j, b + 1))
                act.activation(PT[s][0][:, 2 * b:2 * b + 2, :], bank[s][b][:], ACT.Copy,
                               scale=PT_SCALE / H_SCALE).then_inc(pth_done[s], 1)

            def q_k(s, j, layer, n):
                act.wait_ge(qk_done[s], qk_done.at(j, 1))
                act.activation(qk[s][:], bank[s][2][:, 0:2 * NT], ACT.Copy,
                               scale=qk_unscale[:]).then_inc(qkc_done[s], 1)

            def u_v(s, j, layer, n):
                act.wait_ge(Q_done[s], Q_done.at(j, 1))
                act.activation(ea[s][:], qd[s][:], ACT.Exp)
                act.activation(eb[s][:], qd[s][:], ACT.Exp, scale=SLOPE)
                act.activation(r12[s][:, 0, :], bank[s][3][:], ACT.Relu, scale=-1.0, bias=nQ[s][:])
                act_chain.link(act, act.activation(r12[s][:, 1, :], bank[s][3][:], ACT.Relu, bias=Q[s][:]), s, j)
                act.activation(uv[s][:], r12[s][:], ACT.Exp, scale=SLOPE - 1.0).then_inc(uv_done[s], 1)

            def exp_v(s, j, layer, nt):
                if nt == 0:
                    act.wait_ge(uv_done[s], uv_done.at(j, 1))
                if nt > 1:
                    act.wait_ge(e_done[s], e_done.at(j, nt - 1))
                act.activation(tmp[s][:, nt % 2, :], uv[s][:, 1, :], ACT.Copy,
                               scale=eb[s][:, nt:nt + 1]).then_inc(ev_done[s], 1)

            def e_hi(s, j, layer, nt):
                act.wait_ge(e_done[s], e_done.at(j, nt + 1))
                act.activation(E16[s][0][:, nt, :], E[s][:, nt, :], ACT.Copy, scale=E_SCALE).then_inc(eh_done[s], 1)

            def sums_row(s, j, layer, n):
                act.wait_ge(rsr_done[s], rsr_done.at(j, 1))
                act.activation(rsx[s][:], bank[s][3][:], ACT.Copy).then_inc(rsx_done[s], 1)

            def attended(s, j, layer, ot):
                act.wait_ge(om_done[s], om_done.at(j, ot + 1))
                act.activation(orl[s][:, ot, :], orl[s][:, ot, :], ACT.Relu, scale=l0_unscale[:],
                               bias=bm_col[:, ot:ot + 1]).then_inc(orl_done[s], 1)

            def turned_hi(s, j, layer, b):
                act.wait_ge(hT_ps[s], hT_ps.at(j, 2 * (layer // 2) + b + 1))
                act.activation(hT[s][0][:, 2 * b:2 * b + 2, :], bank[s][b][:], ACT.Relu).then_inc(hTh_done[s], 1)

            def project_hi(which):
                def step(s, j, layer, half):
                    z, b0, k = (zg, 2, 0) if which == "grav" else (zl, 0, 2)
                    act.wait_ge(z_ps[s], z_ps.at(j, 4 * (layer // 2) + k + half + 1))
                    act.activation(z[s][0][:, 2 * half:2 * half + 2, :], bank[s][b0 + half][:], ACT.Copy,
                                   scale=1.0 / H_SCALE).then_inc(zh_done[s], 1)
                return step

            def block_01(which):
                def step(s, j, layer, n):
                    ps, k = (gg_ps, 0) if which == "grav" else (gl_ps, 1)
                    act.wait_ge(ps[s], ps.at(j, layer // 2 + 1))
                    act.activation(g01[s][:, k, :], bank[s][2 + k][:, P:2 * P], ACT.Copy).then_inc(g01_done[s], 1)
                return step

            def lang_relu(s, j, layer, n):
                act.wait_ge(rl_ps[s], rl_ps.at(j, layer // 2 + 1))
                for nt in range(CT):
                    a = act.activation(tl[s][:, nt, :], bank[s][3][:, nt * C:(nt + 1) * C], ACT.Relu,
                                       scale=rsl[s][:, nt:nt + 1])
                a.then_inc(tl_done[s], 1)

            def squares_row(s, j, layer, n):
                act.wait_ge(rg_ps[s], rg_ps.at(j, layer // 2 + 1))
                act.activation(sqr[s][:], bank[s][0][:, C:2 * C], ACT.Copy, scale=-0.5).then_inc(sqr_done[s], 1)

            def gauss(s, j, layer, n):
                li = layer // 2
                act.wait_ge(e0_done[s], e0_done.at(j, li + 1))
                act.wait_ge(bg_done[s], bg_done.at(j, li + 1))
                for nt in range(CT):
                    a = act.activation(Eg[s][:, nt, :], e0[s][:, nt, :], ACT.Exp, scale=two_c[:, li:li + 1],
                                       bias=bg[s][:, nt:nt + 1])
                a.then_inc(eg_done[s], 1)

            def lang_normed(s, j, layer, n):
                act.wait_ge(rdl_done[s], rdl_done.at(j, layer // 2 + 1))
                for nt in range(CT):
                    a = act.activation(tl[s][:, nt, :], Bl[s][:, nt, :], ACT.Copy, scale=rdeg[s][:, 0, nt:nt + 1])
                a.then_inc(kl_done[s], 1)

            def values_hi(s, j, layer, half):
                act.wait_ge(v_ps[s], v_ps.at(j, 2 * (layer // 2) + half + 1))
                act.activation(vv[s][0][:, half, :], bank[s][1 + half][:], ACT.Copy,
                               scale=1.0 / H_SCALE).then_inc(vh_done[s], 1)

            def k_hi(s, j, layer, n):
                act.wait_ge(kt_ps[s], kt_ps.at(j, layer // 2 + 1))
                act.activation(KT[s][0][:], bank[s][3][:], ACT.Copy).then_inc(kth_done[s], 1)

            def store(s, j, layer, n):
                act.wait_ge(x4_done[s], x4_done.at(j, 2))
                act.dma_start(out_dram[2 * j + s], xs[s][:]).then_inc(x_stored[s], 16)
                act_chain.end_sample(s)

            def gate_exp(s, j, layer, n):
                act.wait_ge(c_landed, LOADS)
                act.activation(small[:, 0:2], gl[:, 0:2], ACT.Exp, scale=-1.0).then_inc(prep_exp, 1)
                act.activation(small[:, 2:4], gl[:, 2:4], ACT.Exp).then_inc(prep_exp, 1)

            def adj_split_hi(s, j, layer, n):
                act.wait_ge(scaled, 1)
                act.activation(wqk[0][:], wqk_f[:], ACT.Copy, scale=s_of("qk")).then_inc(adj_hi, 1)
                act.wait_ge(adj_turned, 1)
                act.activation(adjT[0][:], bank[0][0][:], ACT.Copy, scale=s_of("adj")).then_inc(adj_hi, 1)
                act.wait_ge(squared, 2)
                act.activation(adj2[0][:], tl[0][:], ACT.Copy).then_inc(adj_hi, 1)

            def matrix_copy(s, j, job, n):
                to = wo_t if JOBS[job][1] == "keep" else product_f
                for dt in range(DT):
                    act.wait_ge(tile_ps, job * DT + dt + 1)
                    act.activation(to[dt // 2][:, dt % 2, :], tile_bank(job * DT + dt)[:], ACT.Copy).then_inc(copied, 1)

            def matrix_hi(s, j, job, n):
                how, name = JOBS[job][1:]
                act.wait_ge(scaled, set_of(name) + 1)
                if how == "multiply":
                    act.wait_ge(copied, copies(job + 1))
                for dt in range(DT):
                    if how == "turn":
                        act.wait_ge(tile_ps, job * DT + dt + 1)
                        src = tile_bank(job * DT + dt)[:]
                    else:
                        src = product_f[dt // 2][:, dt % 2, :]
                    act.activation(weight[name[:-1], int(name[-1])][0][:, dt, :], src, ACT.Copy,
                                   scale=s_of(name)).then_inc(w_hi, 1)

            run(act, "act", {"EX": gate_exp, "AD": adj_split_hi, "CO": matrix_copy, "HI": matrix_hi,
                             "H": h_hi, "AH": adj_h_hi, "QK": q_k, "UV": u_v, "EV": exp_v, "EH": e_hi, "SR": sums_row,
                             "AT": attended, "T": turned_hi, "L": project_hi("lang"), "G": project_hi("grav"),
                             "CL": block_01("lang"), "CG": block_01("grav"), "RL": lang_relu, "SQ": squares_row,
                             "EG": gauss, "KL": lang_normed, "V": values_hi, "KT": k_hi, "ST": store})
            for s in range(2):
                act.wait_ge(x_stored[s], x_stored.at(PAIRS, 0))

        @block.vector
        def _(dve):
            def source(s, layer):
                return xin[s] if layer == 0 else xs[s]

            def statistics(s, j, layer, n):
                if layer == 0:
                    dve.wait_ge(xin_landed[s], xin_landed.at(j, 1))
                for ct in range(CT):
                    a = dve.bn_stats(stats[s][:, ct, :], source(s, layer)[:, ct, :])
                dve_chain.link(dve, a, s, j)
                dve.tensor_copy(carry[s][:], stats[s][:, 0, 0:1])
                for ct in range(CT):
                    a = dve.bn_aggr(mv[s][:, ct, :], stats[s][:, ct, :])
                dve_chain.link(dve, a, s, j)
                dve.tensor_scalar(var_in[s][:], mv[s][:, :, 1], LN_EPS, 1.0 / (H_SCALE * H_SCALE),
                                  ALU.add, ALU.mult).then_inc(stats_done[s], 1)

            def normalise(s, j, layer, n):
                dve.wait_ge(rstd_done[s], rstd_done.at(j, layer + 1))
                for ct in range(CT):
                    dve.tensor_scalar(t_ln[s][:, ct, :], source(s, layer)[:, ct, :], mv[s][:, ct, 0:1],
                                      rstd[s][:, ct:ct + 1], ALU.subtract, ALU.mult).then_inc(t_done[s], 1)

            def h_lo(s, j, layer, ct):
                dve.wait_ge(hh_done[s], hh_done.at(j, layer + ct + 1))
                dve.scalar_tensor_tensor(h[s][1][:, ct, :], t_ln[s][:, ct, :], 0.0, h[s][0][:, ct, :],
                                         ALU.max, ALU.subtract).then_inc(hl_done[s], 1)

            def adj_h_lo(s, j, layer, b):
                dve.wait_ge(pth_done[s], pth_done.at(j, b + 1))
                dve.scalar_tensor_tensor(PT[s][1][:, 2 * b:2 * b + 2, :], bank[s][b][:], PT_SCALE / H_SCALE,
                                         PT[s][0][:, 2 * b:2 * b + 2, :], ALU.mult, ALU.subtract).then_inc(ptl_done[s], 1)

            def q_max(s, j, layer, n):
                dve.wait_ge(qkc_done[s], qkc_done.at(j, 1))
                dve.tensor_reduce(qm[s][:], qk[s][:, :, 0], AX_X, ALU.max).then_inc(qm_done[s], 1)

            def q_less(s, j, layer, n):
                dve.wait_ge(qmr_done[s], qmr_done.at(j, 1))
                dve_chain.link(dve, dve.tensor_reduce(Q[s][:], bank[s][2][:, P:2 * P], AX_X, ALU.max), s, j)
                dve.tensor_scalar(nQ[s][:], Q[s][:], -1.0, None, ALU.mult)
                dve.tensor_scalar(qd[s][:], qk[s][:, :, 0], Q[s][:], None, ALU.subtract).then_inc(Q_done[s], 1)

            def exponentials(s, j, layer, nt):
                if nt < NT:
                    dve.wait_ge(ev_done[s], ev_done.at(j, nt + 1))
                    dve.scalar_tensor_tensor(E[s][:, nt, :], uv[s][:, 0, :], ea[s][:, nt:nt + 1],
                                             tmp[s][:, nt % 2, :], ALU.mult, ALU.max).then_inc(e_done[s], 1)
                if nt > 0:
                    dve.wait_ge(eh_done[s], eh_done.at(j, nt))
                    dve.scalar_tensor_tensor(E16[s][1][:, nt - 1, :], E[s][:, nt - 1, :], E_SCALE,
                                             E16[s][0][:, nt - 1, :], ALU.mult, ALU.subtract).then_inc(el_done[s], 1)

            def sums(s, j, layer, n):
                dve.wait_ge(scol_done[s], scol_done.at(j, 1))
                dve.reciprocal(rs0[s][:], bank[s][2][:, 0:NT]).then_inc(rs0_done[s], 1)

            def attended(s, j, layer, ot):
                dve.wait_ge(rsx_done[s], rsx_done.at(j, 1))
                dve.wait_ge(out_done[s], out_done.at(j, 1))
                dve.tensor_tensor(orl[s][:, ot, :], bank[s][ot][:], rsx[s][:], ALU.mult).then_inc(om_done[s], 1)

            def add_0(s, j, layer, ot):
                if later(j) and ot == 0:
                    dve.wait_ge(x_stored[s], x_stored.at(j, 0))
                dve.wait_ge(orl_done[s], orl_done.at(j, ot + 1))
                dve.tensor_tensor(xs[s][:, ot, :], orl[s][:, ot, :], xin[s][:, ot, :], ALU.add).then_inc(x1_done[s], 1)
                if ot == CT - 1:
                    dve.wait_ge(x1_done[s], x1_done.at(j, CT))

            def turned_lo(s, j, layer, b):
                dve.wait_ge(hTh_done[s], hTh_done.at(j, 2 * (layer // 2) + b + 1))
                dve.scalar_tensor_tensor(hT[s][1][:, 2 * b:2 * b + 2, :], bank[s][b][:], 0.0,
                                         hT[s][0][:, 2 * b:2 * b + 2, :], ALU.max, ALU.subtract).then_inc(hTl_done[s], 1)

            def project_lo(which):
                def step(s, j, layer, half):
                    z, b0, k = (zg, 2, 0) if which == "grav" else (zl, 0, 2)
                    dve.wait_ge(zh_done[s], zh_done.at(j, 4 * (layer // 2) + k + half + 1))
                    dve.scalar_tensor_tensor(z[s][1][:, 2 * half:2 * half + 2, :], bank[s][b0 + half][:], 1.0 / H_SCALE,
                                             z[s][0][:, 2 * half:2 * half + 2, :],
                                             ALU.mult, ALU.subtract).then_inc(zlo_done[s], 1)
                return step

            def diagonal(s, k, of):
                for nt in range(CT):
                    a = dve.scalar_tensor_tensor(diag[s][:, k, nt, :], bank[s][2 + k][:, nt * (C + P):nt * (C + P) + P],
                                                 1.0, ident[:], ALU.mult, ALU.mult, accum_out=of[s][:, nt:nt + 1])
                return a

            def lang_norms(s, j, layer, n):
                li = layer // 2
                dve.wait_ge(g01_done[s], g01_done.at(j, 2 * li + 2))
                dve_chain.link(dve, diagonal(s, 1, dgl), s, j)
                dve.tensor_scalar(nrm[s][:], dgl[s][:], norm_floor[:, li:li + 1], None, ALU.max).then_inc(dgl_done[s], 1)

            def grav_norms(s, j, layer, n):
                li = layer // 2
                dve.wait_ge(g01_done[s], g01_done.at(j, 2 * li + 1))
                diagonal(s, 0, dgg).then_inc(dgg_done[s], 1)
                dve.wait_ge(dgg_done[s], dgg_done.at(j, li + 1))
                dve.tensor_scalar(bg[s][:], dgg[s][:], neg_c[:, li:li + 1], None, ALU.mult).then_inc(bg_done[s], 1)

            def inverse_degrees(s, j, li, k):
                dve_chain.link(dve, dve.tensor_scalar(deg[s][:, k, :], deg[s][:, k, :], EPS, None, ALU.max), s, j)
                dve_chain.link(dve, dve.reciprocal(deg[s][:, k, :], deg[s][:, k, :]), s, j)
                return dve.tensor_scalar(rdeg[s][:, k, :], deg[s][:, k, :], gates[:, li, k:k + 1], None, ALU.mult)

            def lang_kernel(s, j, layer, n):
                li = layer // 2
                dve.wait_ge(tl_done[s], tl_done.at(j, li + 1))
                row = bank[s][0][:, 0:C].unsqueeze(1).to_broadcast((P, CT, C))
                dve.tensor_tensor(tl[s][:], tl[s][:], row, ALU.mult).then_inc(row_used[s], 1)
                dve.wait_ge(row_used[s], row_used.at(j, li + 1))
                for nt in range(CT):
                    a = dve.scalar_tensor_tensor(Bl[s][:, nt, :], tl[s][:, nt, :], 1.0, adj_off[:, nt, :],
                                                 ALU.mult, ALU.mult, accum_out=deg[s][:, 0, nt:nt + 1])
                dve_chain.link(dve, a, s, j)
                inverse_degrees(s, j, li, 0).then_inc(rdl_done[s], 1)

            def grav_exponent(s, j, layer, n):
                li = layer // 2
                dve.wait_ge(sqr_done[s], sqr_done.at(j, li + 1))
                dve.tensor_tensor(e0[s][:], bank[s][2][:].rearrange("p (t c) -> p t c", t=CT),
                                  sqr[s][:].unsqueeze(1).to_broadcast((P, CT, C)), ALU.add).then_inc(e0_done[s], 1)

            def grav_kernel(s, j, layer, n):
                li = layer // 2
                dve.wait_ge(eg_done[s], eg_done.at(j, li + 1))
                for nt in range(CT):
                    a = dve.scalar_tensor_tensor(Bg[s][:, nt, :], Eg[s][:, nt, :], 1.0, adj_off[:, nt, :],
                                                 ALU.min, ALU.mult, accum_out=deg[s][:, 1, nt:nt + 1])
                dve_chain.link(dve, a, s, j)
                dve_chain.link(dve, inverse_degrees(s, j, li, 1), s, j)

            def mixture(s, j, layer, n):
                li = layer // 2
                dve.wait_ge(kl_done[s], kl_done.at(j, li + 1))
                for nt in range(CT):
                    a = dve.scalar_tensor_tensor(Km[s][:, nt, :], Bg[s][:, nt, :], rdeg[s][:, 1, nt:nt + 1],
                                                 tl[s][:, nt, :], ALU.mult, ALU.add)
                a.then_inc(K_done[s], 1)

            def values_lo(s, j, layer, half):
                dve.wait_ge(vh_done[s], vh_done.at(j, 2 * (layer // 2) + half + 1))
                dve.scalar_tensor_tensor(vv[s][1][:, half, :], bank[s][1 + half][:], 1.0 / H_SCALE, vv[s][0][:, half, :],
                                         ALU.mult, ALU.subtract).then_inc(vl_done[s], 1)

            def k_lo(s, j, layer, n):
                dve.wait_ge(kth_done[s], kth_done.at(j, layer // 2 + 1))
                dve.tensor_tensor(KT[s][1][:], bank[s][3][:].rearrange("p (t c) -> p t c", t=CT), KT[s][0][:],
                                  ALU.subtract).then_inc(ktl_done[s], 1)

            def add_1_3(s, j, layer, nt):
                li = layer // 2
                done = x2_done if layer == 1 else x4_done
                dve.wait_ge(y_ps[s], y_ps.at(j, (0 if layer == 1 else 4) + nt + 1))
                dve.scalar_tensor_tensor(xs[s][:, nt, :], bank[s][nt][:], v_unscale[:, li:li + 1], xs[s][:, nt, :],
                                         ALU.mult, ALU.add).then_inc(done[s], 1)
                if layer == 1 and nt == CT - 1:
                    dve.wait_ge(x2_done[s], x2_done.at(j, CT))
                if layer == 3 and nt == CT - 1:
                    dve_chain.end_sample(s)

            def add_2(s, j, layer, mt):
                dve.wait_ge(y_ps[s], y_ps.at(j, 2 + mt + 1))
                dve.wait_ge(xb_done[s], xb_done.at(j, mt + 1))
                dve_chain.link(dve, dve.scalar_tensor_tensor(xs[s][:, mt, :], bank[s][mt][:], l2_unscale[:],
                                                             xb[s][:, mt, :], ALU.mult, ALU.add), s, j)

            prep_steps = [0]

            def link(ins):
                prep_steps[0] += 1
                ins.then_inc(prep_chain, 1)
                dve.wait_ge(prep_chain, prep_steps[0])

            def find_max(s, j, k, n):
                names = SCALE_SETS[k]
                m0 = MATS.index(names[0])
                if k == 0:
                    dve.wait_ge(c_landed, LOADS)
                    dve.tensor_reduce(abs_max[:, 0:1], adj_sb[:].rearrange("p t m -> p (t m)"), AX_X, ALU.max,
                                      apply_absolute_value=True)
                    dve.tensor_reduce(abs_max[:, 1:2], wqk_f[:].rearrange("p t k -> p (t k)"), AX_X, ALU.max,
                                      apply_absolute_value=True).then_inc(max_found, 1)
                    return
                for m, name in enumerate(names, m0):
                    job = [x[2] for x in JOBS].index(name)
                    if JOBS[job][1] == "multiply":
                        dve.wait_ge(copied, copies(job + 1))
                        src = product_f
                    else:
                        dve.wait_ge(w_landed[job % 4], 32 * (job // 4 + 1))
                        src = staging[job % 4]
                    for half in range(2):
                        a = dve.tensor_reduce(part_max[:, m, half:half + 1], src[half].rearrange("p t n -> p (t n)"), AX_X,
                                              ALU.max, apply_absolute_value=True)
                link(a)
                dve.tensor_reduce(abs_max[:, m0:m0 + len(names)], part_max[:, m0:m0 + len(names), :], AX_X,
                                  ALU.max).then_inc(max_found, 1)

            def find_scale(s, j, k, n):
                m0, width = MATS.index(SCALE_SETS[k][0]), len(SCALE_SETS[k])
                a, b = scratch[:, 0, 0:width], scratch[:, 1, 0:width]
                dve.wait_ge(max_row, k + 1)
                link(dve.tensor_reduce(a, bank[1][3][:, 0:width * P].rearrange("p (m c) -> p m c", m=width), AX_X, ALU.max))
                link(dve.tensor_scalar(b.bitcast(U32), a.bitcast(U32), 0x7F800000, None, ALU.bitwise_and))
                link(dve.tensor_scalar(inv[:, m0:m0 + width, 0], b, 2.0 ** -100, 1.0 / W_TOP, ALU.max, ALU.mult))
                dve.reciprocal(scale[:, m0:m0 + width, 0], inv[:, m0:m0 + width, 0]).then_inc(scaled, 1)
                dve.wait_ge(scaled, k + 1)

            def adj_square(s, j, layer, n):
                dve.tensor_scalar(Bl[0][:], adj_sb[:], s_of("adj"), None, ALU.mult).then_inc(squared, 1)
                dve.wait_ge(squared, 1)
                dve.tensor_tensor(tl[0][:], Bl[0][:], Bl[0][:], ALU.mult).then_inc(squared, 1)
                dve.tensor_scalar(qk_unscale[:], i_of("qk"), 1.0 / H_SCALE, None, ALU.mult)
                dve.tensor_scalar(l0_unscale[:], i_of("adj"), 1.0 / (PT_SCALE * E_SCALE), None, ALU.mult)
                dve.scalar_tensor_tensor(l2_unscale[:], i_of("adj"), 1.0 / H_SCALE, i_of("adj"), ALU.mult, ALU.mult)

            def adj_split_lo(s, j, layer, n):
                dve.wait_ge(adj_hi, 1)
                dve.scalar_tensor_tensor(wqk[1][:], wqk_f[:], s_of("qk"), wqk[0][:], ALU.mult, ALU.subtract)
                dve.wait_ge(adj_hi, 2)
                dve.scalar_tensor_tensor(adjT[1][:], bank[0][0][:].rearrange("p (t c) -> p t c", t=CT), s_of("adj"),
                                         adjT[0][:], ALU.mult, ALU.subtract)
                dve.wait_ge(adj_hi, 3)
                dve.wait_ge(squared, 2)
                dve.tensor_tensor(adj2[1][:], tl[0][:], adj2[0][:], ALU.subtract)

            def matrix_lo(s, j, job, n):
                how, name = JOBS[job][1:]
                hi, lo = weight[name[:-1], int(name[-1])]
                for dt in range(DT):
                    dve.wait_ge(w_hi, splits(job) + dt + 1)
                    src = tile_bank(job * DT + dt)[:] if how == "turn" else product_f[dt // 2][:, dt % 2, :]
                    dve.scalar_tensor_tensor(lo[:, dt, :], src, s_of(name), hi[:, dt, :],
                                             ALU.mult, ALU.subtract).then_inc(w_lo, 1)

            def factors(s, j, layer, n):
                li = layer // 2
                col = slice(li, li + 1)
                dve.wait_ge(consts_made, 5)
                dve.wait_ge(prep_exp, 2)
                link(dve.tensor_scalar(small[:, 4:5], small[:, col], 1.0, None, ALU.add))
                link(dve.reciprocal(small[:, 5:6], small[:, 4:5]))
                dve.tensor_scalar(gates[:, li, 0:1], small[:, 5:6], K_SCALE, None, ALU.mult)
                dve.tensor_scalar(gates[:, li, 1:2], small[:, 5:6], -K_SCALE, K_SCALE, ALU.mult, ALU.add)
                sigma = small[:, 2 + li:3 + li]
                link(dve.scalar_tensor_tensor(small[:, 6:7], sigma, 1.0, sigma, ALU.mult, ALU.mult))
                link(dve.reciprocal(small[:, 7:8], small[:, 6:7]))
                ig = i_of(f"grav{layer}")
                link(dve.scalar_tensor_tensor(small[:, 6:7], ig, small[:, 7:8], ig, ALU.mult, ALU.mult))
                dve.tensor_scalar(two_c[:, col], small[:, 6:7], 1.0, None, ALU.mult)
                dve.tensor_scalar(neg_c[:, col], small[:, 6:7], -0.5, None, ALU.mult)
                sl = s_of(f"lang{layer}")
                dve.scalar_tensor_tensor(norm_floor[:, col], sl, EPS * EPS, sl, ALU.mult, ALU.mult)
                dve.tensor_scalar(v_unscale[:, col], i_of(f"vo{layer}"), 1.0 / K_SCALE, None, ALU.mult)

            run(dve, "dve", {"MX": find_max, "SC": find_scale, "SQ": adj_square, "AD": adj_split_lo, "LO": matrix_lo,
                             "FA": factors,
                             "ST": statistics, "N": normalise, "H": h_lo, "AH": adj_h_lo, "QM": q_max, "Q": q_less,
                             "E": exponentials, "SM": sums, "AT": attended, "X": add_0, "T": turned_lo,
                             "L": project_lo("lang"), "G": project_lo("grav"), "DL": lang_norms, "DG": grav_norms,
                             "RL": lang_kernel, "RG": grav_exponent, "BG": grav_kernel, "K": mixture,
                             "V": values_lo, "KT": k_lo, "Y": add_1_3, "S": add_2})

        @block.gpsimd
        def _(pool):
            def deviations(s, j, layer, n):
                pool.wait_ge(stats_done[s], stats_done.at(j, layer + 1))
                pool.tensor_tensor(rstd[s][:], var_in[s][:], minus_half[:], ALU.pow).then_inc(rstd_done[s], 1)

            def add_bias(s, j, layer, ct):
                pool.tensor_tensor(xb[s][:, ct, :], xs[s][:, ct, :], bias_row[:], ALU.add).then_inc(xb_done[s], 1)

            def sum_e(s, j, layer, n):
                pool.wait_ge(e_done[s], e_done.at(j, 2 * n + 2))
                a = pool.tensor_tensor(esum[s][:, n, :], E[s][:, 2 * n, :], E[s][:, 2 * n + 1, :], ALU.add)
                if n == 1:
                    pool_chain.link(pool, a, s, j)
                    pool.tensor_tensor(esum[s][:, 0, :], esum[s][:, 0, :], esum[s][:, 1, :],
                                       ALU.add).then_inc(esum_done[s], 1)

            def inverse_norms(s, j, layer, n):
                pool.wait_ge(dgl_done[s], dgl_done.at(j, layer // 2 + 1))
                pool.tensor_tensor(rsl[s][:], nrm[s][:], minus_half[:], ALU.pow).then_inc(rsl_done[s], 1)
                if layer == 3:
                    pool_chain.end_sample(s)

            def constants(s, j, layer, n):
                pool.memset(ident[:], 0.0).then_inc(consts_made, 1)
                pool.memset(ones[:], 1.0).then_inc(consts_made, 1)
                pool.memset(minus_half[:], -0.5).then_inc(consts_made, 1)
                pool.wait_ge(consts_made, 3)
                pool.affine_select(out=ident[:], in_=ident[:], compare_op=ALU.not_equal, fill=1.0, base=0,
                                   pattern=[[-1, P]], channel_multiplier=1).then_inc(consts_made, 1)

            def off_diagonal(s, j, layer, n):
                pool.wait_ge(c_landed, LOADS)
                pool.affine_select(out=adj_off[:], in_=adj_sb[:], compare_op=ALU.not_equal, fill=0.0, base=0,
                                   pattern=[[P, CT], [-1, C]], channel_multiplier=1).then_inc(consts_made, 1)

            run(pool, "pool", {"CO": constants, "OF": off_diagonal,
                               "ST": deviations, "XB": add_bias, "SE": sum_e, "DL": inverse_norms})


_INS = ["x", "adj", "L0_gnn_wq", "L0_gnn_wk", "L0_gnn_bm",
        "L1_gnn_W_lang", "L1_gnn_W_grav", "L1_gnn_W_V", "L1_gnn_W_O", "L1_gnn_gate_logit", "L1_gnn_log_sigma",
        "L2_gnn_bias",
        "L3_gnn_W_lang", "L3_gnn_W_grav", "L3_gnn_W_V", "L3_gnn_W_O", "L3_gnn_gate_logit", "L3_gnn_log_sigma"]


def kernel(**inputs):
    import numpy as _np
    import concourse.bacc as _bacc
    from concourse import mybir as _mybir
    from concourse.bass_utils import run_bass_kernel_spmd as _run

    nc = _bacc.Bacc("TRN2", target_bir_lowering=False, num_devices=1)
    arrays, args = {}, []
    for name in _INS:
        a = _np.ascontiguousarray(inputs[name])
        if a.ndim == 0 or a.size == 1:
            a = a.reshape(1, 1)
        arrays[f"in_{name}"] = a
        args.append(nc.dram_tensor(f"in_{name}", a.shape, _mybir.dt.from_np(a.dtype), kind="ExternalInput").ap())
    shape = inputs["x"].shape
    out = nc.dram_tensor("out_0", shape, _mybir.dt.float32, kind="ExternalOutput").ap()
    build(nc, *args, out)
    r = _run(nc, [arrays], core_ids=[0])
    return r.results[0]["out_0"]
```

```python
from contextlib import ExitStack

import concourse.bass as bass
from concourse import mybir

F32 = mybir.dt.float32
F16 = mybir.dt.float16
U32 = mybir.dt.uint32
ALU = mybir.AluOpType
ACT = mybir.ActivationFunctionType
AX_X = mybir.AxisListType.X

P = 128
DVE_STEPS, ACT_STEPS, POOL_STEPS = 27, 1, 1
LN_EPS = 1e-5
EPS = 1e-8
SLOPE = 0.01

H_SCALE = 256.0
W_TOP = 8.0
PT_SCALE = 0.5
E_SCALE = 16384.0
K_SCALE = 1024.0

ORDER = {
    "pe": """
        W0AD b3G1 W0MR A0AH b3L0 W1MR W0TU W1TU W2TU A0QK W3PR0 b3L1 W3PR1 W3PR2 b3GG W3PR3 b3GL b3RG A0AT0
        A0AT1 b3RL A0AT2 W2MR A0AT3 A0SM A0SR W3MR b3V0 b3V1 W4TU W5TU b3V2 b3V3 W6TU b3KT A1T b3Y0 W7PR0 b3Y1
        W7PR1 W7PR2 W7PR3 A1G0 W4MR A1G1 B0AH A1L0 B0QK A1L1 A1GG A1GL A1RG B0AT0 B0AT1 A1RL B0AT2 B0AT3 B0SM
        B0SR A1V0 A1V1 A1KT A1V2 A1V3 B1T A1Y0 B1G0 A1Y1 B1G1 B1L0 B1L1 A2S B1GG B1GL B1RG B1V0 B1V1 B1RL A3T
        B1V2 B1V3 A3G0 B1KT A3G1 B1Y0 B1Y1 A3L0 A3L1 A3GG B2S A3GL A3RG A3V0 A3RL A3V1 B3T A3V2 A3V3 A3KT A3Y0
        A3Y1 B3G0""",
    "act": """
        W0EX W0AD A0H0 A0H1 b3G0 b3G1 A0AH0 A0QK W0HI W1HI A0AH1 W2CO b3L0 A0UV A0EV0 b3L1 A0EV1 b3CG A0EH0
        A0EV2 A0EH1 A0EV3 b3CL A0EH2 b3SQ W3CO A0EH3 b3RL W3HI b3EG A0SR b3KL A0AT0 A0AT1 b3V0 W4HI W5HI W6CO
        b3V1 b3KT A1T0 A1T1 W7CO A1G0 W7HI b3ST B0H0 B0H1 B0AH0 B0AH1 A1G1 B0QK A1L0 B0UV A1L1 B0EV0 A1CG B0EV1
        B0EH0 B0EV2 B0EH1 A1CL B0EV3 B0EH2 A1SQ B0EH3 A1RL A1EG A1KL B0SR B0AT0 B0AT1 A1KT A1V0 A1V1 B1T0 B1T1
        B1G0 B1G1 A2H0 A2H1 B1L0 B1L1 B1CG B1CL B1SQ B1RL A3T0 B1EG A3T1 B1KL B1V0 B1V1 B1KT A3G0 A3G1 A3L0
        B2H0 B2H1 A3L1 A3CG A3CL A3SQ A3RL A3EG B3T0 A3V0 A3KL B3T1 A3V1 A3KT A3ST""",
    "dve": """
        W0MX A0BS0 A0BS1 A0ST W0SC A0N W0SQ W0AD A0H0 A0H1 W1MX W1SC W0LO W1LO A0AH0 A0QM b3G0 A0Q b3G1 A0AH1
        b3L0 A0E0 b3L1 b3DG A0E1 A0E2 b3DL A0E3 b3RG W2MX A0E4 W2SC W1FA b3RL A0SM b3BG W3LO A0AT0 A0AT1 b3K
        W3MX A0X0 A0X1 A1BS0 A1BS1 W3SC A1ST b3V0 W4LO W5LO A1N b3V1 b3KT A1T0 A1T1 W4MX W4SC b3Y0 W3FA W7LO
        b3Y1 B0BS0 B0BS1 B0ST B0N B0H0 B0H1 B0QM B0AH0 A1G0 B0Q A1G1 A1L0 B0AH1 A1L1 B0E0 A1DG B0E1 B0E2 A1DL
        B0E3 A1RG B0E4 A1RL B0SM A1BG B0AT0 B0AT1 A1K B0X0 B0X1 B1BS0 B1BS1 B1ST A1V0 B1N A1V1 B1T0 B1T1 A1KT
        A1Y0 A1Y1 A2BS0 B1G0 B1G1 A2BS1 A2ST A2N A2H0 A2H1 B1L0 A2S0 A3BS0 B1L1 A2S1 A3BS1 B1DG A3ST B1DL B1RG
        A3N B1RL A3T0 A3T1 B1BG B1K B1V0 B1KT B1V1 B1Y0 B2BS0 B1Y1 B2BS1 A3G0 B2ST A3G1 B2N A3L0 B2H0 A3L1 B2H1
        A3DG B2S0 B2S1 B3BS0 B3BS1 A3DL B3ST A3RG B3N A3RL A3BG A3K A3V0 A3V1 A3KT B3T0 B3T1 A3Y0 A3Y1""",
    "pool": """
        W0CO W0OF A0ST A0SE0 b3DL A0SE1 A1ST B0ST B0SE0 A1DL B0SE1 B1ST A2ST A2XB0 A2XB1 B1DL A3ST B2ST B2XB0
        B2XB1 A3DL B3ST""",
    "load": """
        W0C A0X W0M W1M W2M W3M B0X W4M W5M W6M W7M""",
}

class Signal:

    def __init__(self, ctx, nc, name, per, unit=1):
        self.sems = [ctx.enter_context(nc.semaphore(f"{name}_{'ab'[s]}")) for s in range(2)]
        self.per, self.unit = per, unit

    def __getitem__(self, slot):
        return self.sems[slot]

    def at(self, sample, n):
        return sample * (self.per * self.unit) + n * self.unit


class Chain(Signal):

    def __init__(self, ctx, nc, name, per):
        super().__init__(ctx, nc, name, per)
        self.n = [0, 0]

    def link(self, eng, ins, slot, sample):
        self.n[slot] += 1
        ins.then_inc(self[slot], 1)
        eng.wait_ge(self[slot], self.at(sample, self.n[slot]))

    def end_sample(self, slot):
        assert self.n[slot] == self.per, (self.n[slot], self.per)
        self.n[slot] = 0


def later(sample):
    return not isinstance(sample, int) or sample > 0


def build(nc, x, adj, wq, wk, bm, w_lang1, w_grav1, w_v1, w_o1, gate1, sigma1, bias2,
          w_lang3, w_grav3, w_v3, w_o3, gate3, sigma3, out):
    B, C, N = x.shape
    CT, NT, DT = C // P, N // P, N // P
    PAIRS = B // 2
    x_dram = x.rearrange("b (t p) n -> b p t n", p=P)
    out_dram = out.rearrange("b (t p) n -> b p t n", p=P)

    with ExitStack() as ctx:
        def sb(name, shape, dt=F32):
            return ctx.enter_context(nc.sbuf_tensor(name, shape, dt))

        def one(name):
            return ctx.enter_context(nc.semaphore(name))

        def signal(name, per, unit=1):
            return Signal(ctx, nc, name, per, unit)

        ident = sb("ident", [P, P])
        ones = sb("ones", [P, 1])
        minus_half = sb("minus_half", [P, CT])
        adj_sb = sb("adj_sb", [P, CT, C])
        adj_off = sb("adj_off", [P, CT, C])
        adjT = [sb(f"adjT_{p}", [P, CT, C], F16) for p in "hl"]
        adj2 = [sb(f"adj2_{p}", [P, CT, C], F16) for p in "hl"]
        wqk_f = sb("wqk_f", [P, CT, 2])
        wqk = [sb(f"wqk_{p}", [P, CT, 2], F16) for p in "hl"]
        bm_col = sb("bm_col", [P, CT])
        bias_row = sb("bias_row", [P, N])
        weight = {}
        for layer in (1, 3):
            for name in ("lang", "grav", "vo"):
                weight[name, layer] = [sb(f"w_{name}{layer}_{p}", [P, DT, N], F16) for p in "hl"]
        MATS = ["adj", "qk", "lang1", "grav1", "vo1", "lang3", "grav3", "vo3"]
        SCALE_SETS = [["adj", "qk"], ["lang1", "grav1"], ["vo1"], ["lang3", "grav3"], ["vo3"]]
        scale = sb("scale", [P, len(MATS), 1])
        inv = sb("inv", [P, len(MATS), 1])
        part_max = sb("part_max", [P, len(MATS), 2])
        abs_max = sb("abs_max", [P, len(MATS)])
        scratch = sb("scratch", [P, 3, 2])

        def s_of(name):
            return scale[:, MATS.index(name), :]

        def i_of(name):
            return inv[:, MATS.index(name), :]

        qk_unscale = sb("qk_unscale", [P, 1])
        l0_unscale = sb("l0_unscale", [P, 1])
        l2_unscale = sb("l2_unscale", [P, 1])
        gates = sb("gates", [P, 2, 2])
        norm_floor = sb("norm_floor", [P, 2])
        two_c = sb("two_c", [P, 2])
        neg_c = sb("neg_c", [P, 2])
        v_unscale = sb("v_unscale", [P, 2])
        gl = sb("gl", [P, 4])
        small = sb("small", [P, 8])

        def both(name, shape, dt=F32):
            return [sb(f"{name}_{c}", shape, dt) for c in "ab"]

        def both2(name, shape):
            return [[sb(f"{name}{p}_{c}", shape, F16) for p in "hl"] for c in "ab"]

        xin = both("xin", [P, CT, N])
        xs = both("xs", [P, CT, N])
        t_ln = both("t_ln", [P, CT, N])
        xb = both("xb", [P, CT, N])
        stats = both("stats", [P, CT, 6])
        mv = both("mv", [P, CT, 2])
        var_in = both("var_in", [P, CT])
        rstd = both("rstd", [P, CT])
        h = both2("h", [P, CT, N])
        PT = both2("PT", [P, NT, C])
        qk = both("qk", [P, NT, 2])
        qm = both("qm", [P, 1])
        Q = both("Q", [P, 1])
        nQ = both("nQ", [P, 1])
        qd = both("qd", [P, NT])
        ea = both("ea", [P, NT])
        eb = both("eb", [P, NT])
        r12 = both("r12", [P, 2, N])
        uv = both("uv", [P, 2, N])
        tmp = both("tmp", [P, 2, N])
        E = both("E", [P, NT, N])
        E16 = both2("E", [P, NT, N])
        esum = both("esum", [P, 2, N])
        rs0 = both("rs0", [P, NT])
        rsx = both("rsx", [P, N])
        orl = r12
        hT = both2("hT", [P, DT, C])
        zl = both2("zl", [P, DT, C])
        zg = both2("zg", [P, DT, C])
        vv = [[e[:, 0:CT, :] for e in E16[s]] for s in range(2)]
        KT = [[e[:, CT, :].rearrange("p (t c) -> p t c", t=CT) for e in E16[s]] for s in range(2)]

        def tile_of(buf, n):
            return [buf[s][:, n, :].rearrange("p (t c) -> p t c", t=CT) for s in range(2)]

        diag = both("diag", [P, 2, CT, P])
        carry = both("carry", [P, 1])
        dgl = both("dgl", [P, CT])
        dgg = both("dgg", [P, CT])
        nrm = both("nrm", [P, CT])
        rsl = both("rsl", [P, CT])
        bg = both("bg", [P, CT])
        sqr = both("sqr", [P, C])
        g01 = [uv[s][:, 0, 0:2 * P].rearrange("p (k m) -> p k m", k=2) for s in range(2)]
        tl = tile_of(E, 0)
        Bl = tile_of(E, 1)
        e0 = tile_of(E, 2)
        Eg = tile_of(E, 3)
        Bg = tile_of(xb, 0)
        deg = both("deg", [P, 2, CT])
        rdeg = both("rdeg", [P, 2, CT])
        Km = tile_of(xb, 1)
        bank = [[ctx.enter_context(nc.psum_tensor(f"bank{b}_{c}", [P, 512], F32)) for b in range(4)]
                for c in "ab"]

        xin_landed = signal("xin_landed", 1, 16)
        x_stored = signal("x_stored", 1, 16)
        x1_done = signal("x1_done", 2)
        x2_done = signal("x2_done", 2)
        x4_done = signal("x4_done", 2)
        xb_done = signal("xb_done", 2)
        stats_done = signal("stats_done", 4)
        rstd_done = signal("rstd_done", 4)
        t_done = signal("t_done", 8)
        hh_done = signal("hh_done", 4)
        hl_done = signal("hl_done", 4)
        pt_done = signal("pt_done", 2)
        pth_done = signal("pth_done", 2)
        ptl_done = signal("ptl_done", 2)
        qk_done = signal("qk_done", 1)
        qkc_done = signal("qkc_done", 1)
        qm_done = signal("qm_done", 1)
        qmr_done = signal("qmr_done", 1)
        Q_done = signal("Q_done", 1)
        uv_done = signal("uv_done", 1)
        ev_done = signal("ev_done", 4)
        e_done = signal("e_done", 4)
        eh_done = signal("eh_done", 4)
        el_done = signal("el_done", 4)
        esum_done = signal("esum_done", 1)
        out_done = signal("out_done", 1)
        scol_done = signal("scol_done", 1)
        rs0_done = signal("rs0_done", 1)
        rsr_done = signal("rsr_done", 1)
        rsx_done = signal("rsx_done", 1)
        om_done = signal("om_done", 2)
        orl_done = signal("orl_done", 2)
        hT_ps = signal("hT_ps", 4)
        hTh_done = signal("hTh_done", 4)
        hTl_done = signal("hTl_done", 4)
        z_ps = signal("z_ps", 8)
        zh_done = signal("zh_done", 8)
        zlo_done = signal("zlo_done", 8)
        gl_ps = signal("gl_ps", 2)
        gg_ps = signal("gg_ps", 2)
        dgl_done = signal("dgl_done", 2)
        dgg_done = signal("dgg_done", 2)
        g01_done = signal("g01_done", 4)
        rsl_done = signal("rsl_done", 2)
        bg_done = signal("bg_done", 2)
        rl_ps = signal("rl_ps", 2)
        row_used = signal("row_used", 2)
        rg_ps = signal("rg_ps", 2)
        sqr_done = signal("sqr_done", 2)
        tl_done = signal("tl_done", 2)
        e0_done = signal("e0_done", 2)
        eg_done = signal("eg_done", 2)
        rdl_done = signal("rdl_done", 2)
        kl_done = signal("kl_done", 2)
        K_done = signal("K_done", 4)
        v_ps = signal("v_ps", 4)
        vh_done = signal("vh_done", 4)
        vl_done = signal("vl_done", 4)
        kt_ps = signal("kt_ps", 2)
        kth_done = signal("kth_done", 2)
        ktl_done = signal("ktl_done", 2)
        y_ps = signal("y_ps", 6)
        dve_chain = Chain(ctx, nc, "dve_chain", DVE_STEPS)
        act_chain = Chain(ctx, nc, "act_chain", ACT_STEPS)
        pool_chain = Chain(ctx, nc, "pool_chain", POOL_STEPS)

        staging = [[E[1][:, 0:2, :], E[1][:, 2:4, :]], [t_ln[1][:], xb[1][:]], [r12[1][:], uv[1][:]],
                   [tmp[1][:], esum[1][:]]]
        wo_t = [xs[1], xb[0]]
        product_f = staging[2]
        LOADS = 16 * 9
        w_landed = [one(f"w_landed_{k}") for k in range(4)]
        c_landed = one("c_landed")
        consts_made = one("consts_made")
        max_found = one("max_found")
        max_row = one("max_row")
        scaled = one("scaled")
        adj_turned = one("adj_turned")
        adj_hi = one("adj_hi")
        adj_lo = one("adj_lo")
        squared = one("squared")
        tile_ps = one("tile_ps")
        copied = one("copied")
        w_hi = one("w_hi")
        w_lo = one("w_lo")
        prep_exp = one("prep_exp")
        prep_chain = one("prep_chain")
        JOBS = []
        for layer, wl, wg, wo, wv in ((1, w_lang1, w_grav1, w_o1, w_v1), (3, w_lang3, w_grav3, w_o3, w_v3)):
            JOBS += [(wl, "turn", f"lang{layer}"), (wg, "turn", f"grav{layer}"), (wo, "keep", None),
                     (wv, "multiply", f"vo{layer}")]

        def splits(k):
            return DT * sum(how != "keep" for _, how, _ in JOBS[:k])

        def copies(k):
            return DT * sum(how != "turn" for _, how, _ in JOBS[:k])

        def set_of(name):
            return next(n for n, names in enumerate(SCALE_SETS) if name in names)

        def tile_bank(tile):
            return bank[1][tile % 3]

        def run(eng, name, steps):
            def write(i, slots):
                for step in ORDER[name].split():
                    if step[0] in slots:
                        number = int(step[-1]) if step[-1].isdigit() else 0
                        do = steps[step[2:].rstrip("0123456789")]
                        do(int(step[0] != "A"), i - (step[0] == "b"), int(step[1]), number)

            write(0, "WAB")
            with eng.Fori(1, PAIRS) as i:
                write(i, "bAB")
            write(PAIRS, "b")

        block = ctx.enter_context(nc.Block())

        @block.sync
        def _(sp):
            def load(s, j, layer, n):
                if later(j):
                    sp.wait_ge(x1_done[s], x1_done.at(j, 0))
                sp.dma_start(xin[s][:], x_dram[2 * j + s]).then_inc(xin_landed[s], 16)

            def load_small(s, j, layer, n):
                with nc.allow_non_contiguous_dma(reason="a few small vectors"):
                    sp.dma_start(adj_sb[:], adj.rearrange("(t p) m -> p t m", p=P)).then_inc(c_landed, 16)
                    sp.dma_start(wqk_f[:, :, 0], wq.rearrange("(t p) -> p t", p=P)).then_inc(c_landed, 16)
                    sp.dma_start(wqk_f[:, :, 1], wk.rearrange("(t p) -> p t", p=P)).then_inc(c_landed, 16)
                    sp.dma_start(bm_col[:], bm.rearrange("(t p) -> p t", p=P)).then_inc(c_landed, 16)
                    sp.dma_start(bias_row[:], bias2.partition_broadcast(P)).then_inc(c_landed, 16)
                    for k, a in enumerate((gate1, gate3, sigma1, sigma3)):
                        sp.dma_start(gl[:, k:k + 1], a.to_broadcast((P, 1))).then_inc(c_landed, 16)

            def load_matrix(s, j, job, n):
                if job >= 4:
                    sp.wait_ge(w_lo, splits(min(job - 3, 4)) if job < 6 else splits(4))
                w = JOBS[job][0].rearrange("(t p) n -> p t n", p=P)
                for half in range(2):
                    sp.dma_start(staging[job % 4][half], w[:, 2 * half:2 * half + 2, :]).then_inc(w_landed[job % 4], 16)

            run(sp, "load", {"X": load, "C": load_small, "M": load_matrix})

        @block.tensor
        def _(pe):
            HI_LO = ((0, 0), (0, 1), (1, 0))

            def terms(tiles, late):
                every = [(t, a, b) for t in range(tiles) for a, b in HI_LO]
                lo = [x for x in every if (late != "right" and x[1]) or (late != "left" and x[2])]
                return [x for x in every if x not in lo], lo

            def multiply(to, left, right, sums, start=False, stop=False):
                for n, (t, a, b) in enumerate(sums):
                    mm = pe.matmul(to, left(a, t), right(b, t), start=start and n == 0, stop=stop and n == len(sums) - 1)
                return mm

            def adj_h(s, j, layer, n):
                if later(j):
                    pe.wait_ge(x4_done[s], x4_done.at(j, 0))
                else:
                    pe.wait_ge(adj_lo, 2)
                pe.wait_ge(hh_done[s], hh_done.at(j, 2))
                for nt in range(NT):
                    o = bank[s][nt // 2][:, (nt % 2) * C:(nt % 2 + 1) * C]
                    qo = bank[s][2][:, 2 * nt:2 * nt + 2]
                    hi, lo = terms(CT, "left")
                    left = lambda a, ct: h[s][a][:, ct, nt * P:(nt + 1) * P]
                    multiply(o, left, lambda b, ct: adjT[b][:, ct, :], hi, start=True)
                    multiply(qo, left, lambda b, ct: wqk[b][:, ct, :], hi, start=True)
                    if nt == 0:
                        pe.wait_ge(hl_done[s], hl_done.at(j, 2))
                    mm = multiply(o, left, lambda b, ct: adjT[b][:, ct, :], lo, stop=True)
                    mq = multiply(qo, left, lambda b, ct: wqk[b][:, ct, :], lo, stop=True)
                    if nt % 2 == 1:
                        mm.then_inc(pt_done[s], 1)
                mq.then_inc(qk_done[s], 1)

            def q_k_rows(s, j, layer, n):
                pe.wait_ge(qm_done[s], qm_done.at(j, 1))
                pe.transpose(bank[s][2][:, P:2 * P], qm[s][:, 0:1].to_broadcast((P, P)), ident[:])
                for nt in range(NT):
                    mm = pe.transpose(bank[s][3][:, nt * P:(nt + 1) * P],
                                      qk[s][:, nt, 1:2].to_broadcast((P, P)), ident[:])
                mm.then_inc(qmr_done[s], 1)

            def attend(s, j, layer, nt):
                if nt == 0:
                    pe.wait_ge(ptl_done[s], ptl_done.at(j, 2))
                hi, lo = terms(1, "right")
                left = lambda ot: lambda a, t: PT[s][a][:, nt, ot * P:(ot + 1) * P]
                right = lambda b, t: E16[s][b][:, nt, :]
                pe.wait_ge(eh_done[s], eh_done.at(j, nt + 1))
                for ot in range(CT):
                    multiply(bank[s][ot][:], left(ot), right, hi, start=nt == 0)
                pe.wait_ge(el_done[s], el_done.at(j, nt + 1))
                for ot in range(CT):
                    mm = multiply(bank[s][ot][:], left(ot), right, lo, stop=nt == NT - 1)
                if nt == NT - 1:
                    mm.then_inc(out_done[s], 1)

            def sums(s, j, layer, n):
                pe.wait_ge(esum_done[s], esum_done.at(j, 1))
                for mt in range(NT):
                    mm = pe.matmul(bank[s][2][:, mt:mt + 1], esum[s][:, 0, mt * P:(mt + 1) * P], ones[:],
                                   start=True, stop=True)
                mm.then_inc(scol_done[s], 1)

            def sums_row(s, j, layer, n):
                pe.wait_ge(rs0_done[s], rs0_done.at(j, 1))
                for mt in range(NT):
                    mm = pe.transpose(bank[s][3][:, mt * P:(mt + 1) * P],
                                      rs0[s][:, mt:mt + 1].to_broadcast((P, P)), ident[:])
                mm.then_inc(rsr_done[s], 1)

            def turn(s, j, layer, n):
                for ct in range(CT):
                    pe.wait_ge(t_done[s], t_done.at(j, 2 * layer + ct + 1))
                    for dt in range(DT):
                        mm = pe.transpose(bank[s][dt // 2][:, (dt % 2) * C + ct * P:(dt % 2) * C + (ct + 1) * P],
                                          t_ln[s][:, ct, dt * P:(dt + 1) * P], ident[:])
                        if ct == CT - 1 and dt % 2 == 1:
                            mm.then_inc(hT_ps[s], 1)

            def project(which):
                def step(s, j, layer, half):
                    first = which == "grav" and half == 0
                    li = layer // 2
                    w = weight[which, layer]
                    hi, lo = terms(DT, "right")
                    for e in (0, 1):
                        et = 2 * half + e
                        to = bank[s][(2 if which == "grav" else 0) + half][:, e * C:(e + 1) * C]
                        left = lambda a, dt: w[a][:, dt, et * P:(et + 1) * P]
                        right = lambda b, dt: hT[s][b][:, dt, :]
                        for sums, ready in ((hi, hTh_done), (lo, hTl_done)):
                            for b in (0, 1):
                                if first and e == 0:
                                    pe.wait_ge(ready[s], ready.at(j, 2 * li + b + 1))
                                mm = multiply(to, left, right, sums[b * len(sums) // 2:(b + 1) * len(sums) // 2],
                                              start=sums is hi and b == 0, stop=sums is lo and b == 1)
                    mm.then_inc(z_ps[s], 1)
                return step

            def gram(which):
                def step(s, j, layer, n):
                    li = layer // 2
                    z, to, k, done = ((zg, bank[s][2], 2, gg_ps) if which == "grav" else (zl, bank[s][3], 4, gl_ps))
                    if which == "grav":
                        pe.wait_ge(zlo_done[s], zlo_done.at(j, 4 * li + 1))
                    else:
                        pe.wait_ge(zlo_done[s], zlo_done.at(j, 4 * li + 2))
                    pe.wait_ge(zh_done[s], zh_done.at(j, 4 * li + k))
                    hi, lo = terms(DT, "both")
                    for nt in range(CT):
                        left = lambda a, et: z[s][a][:, et, nt * P:(nt + 1) * P]
                        right = lambda b, et: z[s][b][:, et, nt * P:C]
                        block = to[:, nt * (C + P):(nt + 1) * C]
                        multiply(block, left, right, hi, start=True)
                        if nt == 0:
                            pe.wait_ge(zlo_done[s], zlo_done.at(j, 4 * li + k))
                        mm = multiply(block, left, right, lo, stop=True)
                    mm.then_inc(done[s], 1)
                return step

            def rows(which):
                def step(s, j, layer, n):
                    li = layer // 2
                    src, c0, k, ready, done = ((dgg, C, 0, dgg_done, rg_ps) if which == "grav"
                                               else (rsl, 0, 1, rsl_done, rl_ps))
                    pe.wait_ge(ready[s], ready.at(j, li + 1))
                    pe.wait_ge(g01_done[s], g01_done.at(j, 2 * li + k + 1))
                    pe.transpose(bank[s][2 + k][:, C:C + P], g01[s][:, k, :], ident[:])
                    if which == "lang":
                        pe.wait_ge(sqr_done[s], sqr_done.at(j, li + 1))
                    for mt in range(CT):
                        mm = pe.transpose(bank[s][0][:, c0 + mt * P:c0 + (mt + 1) * P],
                                          src[s][:, mt:mt + 1].to_broadcast((P, P)), ident[:])
                    mm.then_inc(done[s], 1)
                return step

            def values(s, j, layer, quarter):
                half, part = quarter // 2, quarter % 2
                if quarter == 0:
                    pe.wait_ge(zlo_done[s], zlo_done.at(j, 4 * (layer // 2) + 4))
                if quarter == 2:
                    pe.wait_ge(e0_done[s], e0_done.at(j, layer // 2 + 1))
                w = weight["vo", layer]
                for dt in range(part * DT // 2, (part + 1) * DT // 2):
                    for a, b in HI_LO:
                        mm = pe.matmul(bank[s][1 + half][:], hT[s][a][:, dt, half * P:(half + 1) * P], w[b][:, dt, :],
                                       start=dt == 0 and a == b, stop=dt == DT - 1 and a == 1)
                if part == 1:
                    mm.then_inc(v_ps[s], 1)

            def turn_k(s, j, layer, n):
                for nt in range(CT):
                    pe.wait_ge(K_done[s], K_done.at(j, CT * (layer // 2) + nt + 1))
                    for mt in range(CT):
                        mm = pe.transpose(bank[s][3][:, mt * C + nt * P:mt * C + (nt + 1) * P],
                                          Km[s][:, nt, mt * P:(mt + 1) * P], ident[:])
                mm.then_inc(kt_ps[s], 1)

            def apply(s, j, layer, part):
                li = layer // 2
                terms_of = terms(CT, "left")[part]
                if part == 0:
                    pe.wait_ge(vl_done[s], vl_done.at(j, 2 * li + 2))
                    pe.wait_ge(kth_done[s], kth_done.at(j, li + 1))
                else:
                    pe.wait_ge(ktl_done[s], ktl_done.at(j, li + 1))
                for nt in range(CT):
                    mm = multiply(bank[s][nt][:], lambda a, mt: KT[s][a][:, mt, nt * P:(nt + 1) * P],
                                  lambda b, mt: vv[s][b][:, mt, :], terms_of, start=part == 0, stop=part == 1)
                    if part == 1:
                        mm.then_inc(y_ps[s], 1)

            def support(s, j, layer, n):
                pe.wait_ge(hh_done[s], hh_done.at(j, 4))
                hi, lo = terms(CT, "right")
                left = lambda mt: lambda a, nt: adj2[a][:, nt, mt * P:(mt + 1) * P]
                right = lambda b, nt: h[s][b][:, nt, :]
                for mt in range(CT):
                    multiply(bank[s][mt][:], left(mt), right, hi, start=True)
                pe.wait_ge(hl_done[s], hl_done.at(j, 4))
                for mt in range(CT):
                    multiply(bank[s][mt][:], left(mt), right, lo, stop=True).then_inc(y_ps[s], 1)

            def adj_turn(s, j, layer, n):
                pe.wait_ge(c_landed, LOADS)
                pe.wait_ge(consts_made, 4)
                for ct in range(CT):
                    for ot in range(CT):
                        mm = pe.transpose(bank[0][3][:, ct * C + ot * P:ct * C + (ot + 1) * P],
                                          adj_sb[:, ot, ct * P:(ct + 1) * P], ident[:])
                mm.then_inc(adj_turned, 1)

            def max_rows(s, j, k, n):
                pe.wait_ge(consts_made, 4)
                pe.wait_ge(max_found, k + 1)
                if k:
                    pe.wait_ge(scaled, k)
                for i, name in enumerate(SCALE_SETS[k]):
                    m = MATS.index(name)
                    mm = pe.transpose(bank[1][3][:, i * P:(i + 1) * P], abs_max[:, m:m + 1].to_broadcast((P, P)),
                                      ident[:])
                mm.then_inc(max_row, 1)

            def bank_free(tile):
                if tile >= 3:
                    k, dt = divmod(tile - 3, DT)
                    if JOBS[k][1] == "turn":
                        pe.wait_ge(w_lo, splits(k) + dt + 1)
                    else:
                        pe.wait_ge(copied, copies(k) + dt + 1)

            def matrix_turn(s, j, job, n):
                pe.wait_ge(w_landed[job % 4], 32 * (job // 4 + 1))
                for dt in range(DT):
                    bank_free(job * DT + dt)
                    for et in range(DT):
                        mm = pe.transpose(tile_bank(job * DT + dt)[:, et * P:(et + 1) * P],
                                          staging[job % 4][et // 2][:, et % 2, dt * P:(dt + 1) * P], ident[:])
                    mm.then_inc(tile_ps, 1)

            def matrix_product(s, j, job, dt):
                pe.wait_ge(w_landed[job % 4], 32 * (job // 4 + 1))
                pe.wait_ge(copied, copies(job))
                bank_free(job * DT + dt)
                for kt in range(DT):
                    mm = pe.matmul(tile_bank(job * DT + dt)[:],
                                   staging[job % 4][kt // 2][:, kt % 2, dt * P:(dt + 1) * P],
                                   wo_t[kt // 2][:, kt % 2, :], start=kt == 0, stop=kt == DT - 1)
                mm.then_inc(tile_ps, 1)

            run(pe, "pe", {"AD": adj_turn, "MR": max_rows, "TU": matrix_turn, "PR": matrix_product,
                           "AH": adj_h, "QK": q_k_rows, "AT": attend, "SM": sums, "SR": sums_row, "T": turn,
                           "L": project("lang"), "G": project("grav"), "GL": gram("lang"), "GG": gram("grav"),
                           "RL": rows("lang"), "RG": rows("grav"), "V": values, "KT": turn_k, "Y": apply,
                           "S": support})

        @block.scalar
        def _(act):
            def h_hi(s, j, layer, ct):
                act.wait_ge(t_done[s], t_done.at(j, 2 * layer + ct + 1))
                act.activation(h[s][0][:, ct, :], t_ln[s][:, ct, :], ACT.Relu).then_inc(hh_done[s], 1)

            def adj_h_hi(s, j, layer, b):
                act.wait_ge(pt_done[s], pt_done.at(j, b + 1))
                act.activation(PT[s][0][:, 2 * b:2 * b + 2, :], bank[s][b][:], ACT.Copy,
                               scale=PT_SCALE / H_SCALE).then_inc(pth_done[s], 1)

            def q_k(s, j, layer, n):
                act.wait_ge(qk_done[s], qk_done.at(j, 1))
                act.activation(qk[s][:], bank[s][2][:, 0:2 * NT], ACT.Copy,
                               scale=qk_unscale[:]).then_inc(qkc_done[s], 1)

            def u_v(s, j, layer, n):
                act.wait_ge(Q_done[s], Q_done.at(j, 1))
                act.activation(ea[s][:], qd[s][:], ACT.Exp)
                act.activation(eb[s][:], qd[s][:], ACT.Exp, scale=SLOPE)
                act.activation(r12[s][:, 0, :], bank[s][3][:], ACT.Relu, scale=-1.0, bias=nQ[s][:])
                act_chain.link(act, act.activation(r12[s][:, 1, :], bank[s][3][:], ACT.Relu, bias=Q[s][:]), s, j)
                act.activation(uv[s][:], r12[s][:], ACT.Exp, scale=SLOPE - 1.0).then_inc(uv_done[s], 1)

            def exp_v(s, j, layer, nt):
                if nt == 0:
                    act.wait_ge(uv_done[s], uv_done.at(j, 1))
                if nt > 1:
                    act.wait_ge(e_done[s], e_done.at(j, nt - 1))
                act.activation(tmp[s][:, nt % 2, :], uv[s][:, 1, :], ACT.Copy,
                               scale=eb[s][:, nt:nt + 1]).then_inc(ev_done[s], 1)

            def e_hi(s, j, layer, nt):
                act.wait_ge(e_done[s], e_done.at(j, nt + 1))
                act.activation(E16[s][0][:, nt, :], E[s][:, nt, :], ACT.Copy, scale=E_SCALE).then_inc(eh_done[s], 1)

            def sums_row(s, j, layer, n):
                act.wait_ge(rsr_done[s], rsr_done.at(j, 1))
                act.activation(rsx[s][:], bank[s][3][:], ACT.Copy).then_inc(rsx_done[s], 1)

            def attended(s, j, layer, ot):
                act.wait_ge(om_done[s], om_done.at(j, ot + 1))
                act.activation(orl[s][:, ot, :], orl[s][:, ot, :], ACT.Relu, scale=l0_unscale[:],
                               bias=bm_col[:, ot:ot + 1]).then_inc(orl_done[s], 1)

            def turned_hi(s, j, layer, b):
                act.wait_ge(hT_ps[s], hT_ps.at(j, 2 * (layer // 2) + b + 1))
                act.activation(hT[s][0][:, 2 * b:2 * b + 2, :], bank[s][b][:], ACT.Relu).then_inc(hTh_done[s], 1)

            def project_hi(which):
                def step(s, j, layer, half):
                    z, b0, k = (zg, 2, 0) if which == "grav" else (zl, 0, 2)
                    act.wait_ge(z_ps[s], z_ps.at(j, 4 * (layer // 2) + k + half + 1))
                    act.activation(z[s][0][:, 2 * half:2 * half + 2, :], bank[s][b0 + half][:], ACT.Copy,
                                   scale=1.0 / H_SCALE).then_inc(zh_done[s], 1)
                return step

            def block_01(which):
                def step(s, j, layer, n):
                    ps, k = (gg_ps, 0) if which == "grav" else (gl_ps, 1)
                    act.wait_ge(ps[s], ps.at(j, layer // 2 + 1))
                    act.activation(g01[s][:, k, :], bank[s][2 + k][:, P:2 * P], ACT.Copy).then_inc(g01_done[s], 1)
                return step

            def lang_relu(s, j, layer, n):
                act.wait_ge(rl_ps[s], rl_ps.at(j, layer // 2 + 1))
                for nt in range(CT):
                    a = act.activation(tl[s][:, nt, :], bank[s][3][:, nt * C:(nt + 1) * C], ACT.Relu,
                                       scale=rsl[s][:, nt:nt + 1])
                a.then_inc(tl_done[s], 1)

            def squares_row(s, j, layer, n):
                act.wait_ge(rg_ps[s], rg_ps.at(j, layer // 2 + 1))
                act.activation(sqr[s][:], bank[s][0][:, C:2 * C], ACT.Copy, scale=-0.5).then_inc(sqr_done[s], 1)

            def gauss(s, j, layer, n):
                li = layer // 2
                act.wait_ge(e0_done[s], e0_done.at(j, li + 1))
                act.wait_ge(bg_done[s], bg_done.at(j, li + 1))
                for nt in range(CT):
                    a = act.activation(Eg[s][:, nt, :], e0[s][:, nt, :], ACT.Exp, scale=two_c[:, li:li + 1],
                                       bias=bg[s][:, nt:nt + 1])
                a.then_inc(eg_done[s], 1)

            def lang_normed(s, j, layer, n):
                act.wait_ge(rdl_done[s], rdl_done.at(j, layer // 2 + 1))
                for nt in range(CT):
                    a = act.activation(tl[s][:, nt, :], Bl[s][:, nt, :], ACT.Copy, scale=rdeg[s][:, 0, nt:nt + 1])
                a.then_inc(kl_done[s], 1)

            def values_hi(s, j, layer, half):
                act.wait_ge(v_ps[s], v_ps.at(j, 2 * (layer // 2) + half + 1))
                act.activation(vv[s][0][:, half, :], bank[s][1 + half][:], ACT.Copy,
                               scale=1.0 / H_SCALE).then_inc(vh_done[s], 1)

            def k_hi(s, j, layer, n):
                act.wait_ge(kt_ps[s], kt_ps.at(j, layer // 2 + 1))
                act.activation(KT[s][0][:], bank[s][3][:], ACT.Copy).then_inc(kth_done[s], 1)

            def store(s, j, layer, n):
                act.wait_ge(x4_done[s], x4_done.at(j, 2))
                act.dma_start(out_dram[2 * j + s], xs[s][:]).then_inc(x_stored[s], 16)
                act_chain.end_sample(s)

            def gate_exp(s, j, layer, n):
                act.wait_ge(c_landed, LOADS)
                act.activation(small[:, 0:2], gl[:, 0:2], ACT.Exp, scale=-1.0).then_inc(prep_exp, 1)
                act.activation(small[:, 2:4], gl[:, 2:4], ACT.Exp).then_inc(prep_exp, 1)

            def adj_split_hi(s, j, layer, n):
                act.wait_ge(scaled, 1)
                act.activation(wqk[0][:], wqk_f[:], ACT.Copy, scale=s_of("qk")).then_inc(adj_hi, 1)
                act.wait_ge(adj_turned, 1)
                act.activation(adjT[0][:], bank[0][3][:], ACT.Copy, scale=s_of("adj")).then_inc(adj_hi, 1)
                act.wait_ge(squared, 2)
                act.activation(adj2[0][:], tl[0][:], ACT.Copy).then_inc(adj_hi, 1)

            def matrix_copy(s, j, job, n):
                to = wo_t if JOBS[job][1] == "keep" else product_f
                for dt in range(DT):
                    act.wait_ge(tile_ps, job * DT + dt + 1)
                    act.activation(to[dt // 2][:, dt % 2, :], tile_bank(job * DT + dt)[:], ACT.Copy).then_inc(copied, 1)

            def matrix_hi(s, j, job, n):
                how, name = JOBS[job][1:]
                act.wait_ge(scaled, set_of(name) + 1)
                if how == "multiply":
                    act.wait_ge(copied, copies(job + 1))
                for dt in range(DT):
                    if how == "turn":
                        act.wait_ge(tile_ps, job * DT + dt + 1)
                        src = tile_bank(job * DT + dt)[:]
                    else:
                        src = product_f[dt // 2][:, dt % 2, :]
                    act.activation(weight[name[:-1], int(name[-1])][0][:, dt, :], src, ACT.Copy,
                                   scale=s_of(name)).then_inc(w_hi, 1)

            run(act, "act", {"EX": gate_exp, "AD": adj_split_hi, "CO": matrix_copy, "HI": matrix_hi,
                             "H": h_hi, "AH": adj_h_hi, "QK": q_k, "UV": u_v, "EV": exp_v, "EH": e_hi, "SR": sums_row,
                             "AT": attended, "T": turned_hi, "L": project_hi("lang"), "G": project_hi("grav"),
                             "CL": block_01("lang"), "CG": block_01("grav"), "RL": lang_relu, "SQ": squares_row,
                             "EG": gauss, "KL": lang_normed, "V": values_hi, "KT": k_hi, "ST": store})
            for s in range(2):
                act.wait_ge(x_stored[s], x_stored.at(PAIRS, 0))

        @block.vector
        def _(dve):
            def source(s, layer):
                return xin[s] if layer == 0 else xs[s]

            def statistics(s, j, layer, ct):
                if layer == 0:
                    dve.wait_ge(xin_landed[s], xin_landed.at(j, 1))
                elif layer != 3:
                    made = x1_done if layer == 1 else x2_done
                    dve.wait_ge(made[s], made.at(j, ct + 1))
                a = dve.bn_stats(stats[s][:, ct, :], source(s, layer)[:, ct, :])
                if ct == CT - 1:
                    dve_chain.link(dve, a, s, j)

            def mean_and_variance(s, j, layer, n):
                dve.tensor_copy(carry[s][:], stats[s][:, 0, 0:1])
                for ct in range(CT):
                    a = dve.bn_aggr(mv[s][:, ct, :], stats[s][:, ct, :])
                dve_chain.link(dve, a, s, j)
                dve.tensor_scalar(var_in[s][:], mv[s][:, :, 1], LN_EPS, 1.0 / (H_SCALE * H_SCALE),
                                  ALU.add, ALU.mult).then_inc(stats_done[s], 1)

            def normalise(s, j, layer, n):
                dve.wait_ge(rstd_done[s], rstd_done.at(j, layer + 1))
                for ct in range(CT):
                    dve.tensor_scalar(t_ln[s][:, ct, :], source(s, layer)[:, ct, :], mv[s][:, ct, 0:1],
                                      rstd[s][:, ct:ct + 1], ALU.subtract, ALU.mult).then_inc(t_done[s], 1)

            def h_lo(s, j, layer, ct):
                dve.wait_ge(hh_done[s], hh_done.at(j, layer + ct + 1))
                dve.scalar_tensor_tensor(h[s][1][:, ct, :], t_ln[s][:, ct, :], 0.0, h[s][0][:, ct, :],
                                         ALU.max, ALU.subtract).then_inc(hl_done[s], 1)

            def adj_h_lo(s, j, layer, b):
                dve.wait_ge(pth_done[s], pth_done.at(j, b + 1))
                dve.scalar_tensor_tensor(PT[s][1][:, 2 * b:2 * b + 2, :], bank[s][b][:], PT_SCALE / H_SCALE,
                                         PT[s][0][:, 2 * b:2 * b + 2, :], ALU.mult, ALU.subtract).then_inc(ptl_done[s], 1)

            def q_max(s, j, layer, n):
                dve.wait_ge(qkc_done[s], qkc_done.at(j, 1))
                dve.tensor_reduce(qm[s][:], qk[s][:, :, 0], AX_X, ALU.max).then_inc(qm_done[s], 1)

            def q_less(s, j, layer, n):
                dve.wait_ge(qmr_done[s], qmr_done.at(j, 1))
                dve_chain.link(dve, dve.tensor_reduce(Q[s][:], bank[s][2][:, P:2 * P], AX_X, ALU.max), s, j)
                dve.tensor_scalar(nQ[s][:], Q[s][:], -1.0, None, ALU.mult)
                dve.tensor_scalar(qd[s][:], qk[s][:, :, 0], Q[s][:], None, ALU.subtract).then_inc(Q_done[s], 1)

            def exponentials(s, j, layer, nt):
                if nt < NT:
                    dve.wait_ge(ev_done[s], ev_done.at(j, nt + 1))
                    dve.scalar_tensor_tensor(E[s][:, nt, :], uv[s][:, 0, :], ea[s][:, nt:nt + 1],
                                             tmp[s][:, nt % 2, :], ALU.mult, ALU.max).then_inc(e_done[s], 1)
                if nt > 0:
                    dve.wait_ge(eh_done[s], eh_done.at(j, nt))
                    dve.scalar_tensor_tensor(E16[s][1][:, nt - 1, :], E[s][:, nt - 1, :], E_SCALE,
                                             E16[s][0][:, nt - 1, :], ALU.mult, ALU.subtract).then_inc(el_done[s], 1)

            def sums(s, j, layer, n):
                dve.wait_ge(scol_done[s], scol_done.at(j, 1))
                dve.reciprocal(rs0[s][:], bank[s][2][:, 0:NT]).then_inc(rs0_done[s], 1)

            def attended(s, j, layer, ot):
                dve.wait_ge(rsx_done[s], rsx_done.at(j, 1))
                dve.wait_ge(out_done[s], out_done.at(j, 1))
                dve.tensor_tensor(orl[s][:, ot, :], bank[s][ot][:], rsx[s][:], ALU.mult).then_inc(om_done[s], 1)

            def add_0(s, j, layer, ot):
                if later(j) and ot == 0:
                    dve.wait_ge(x_stored[s], x_stored.at(j, 0))
                dve.wait_ge(orl_done[s], orl_done.at(j, ot + 1))
                dve.tensor_tensor(xs[s][:, ot, :], orl[s][:, ot, :], xin[s][:, ot, :], ALU.add).then_inc(x1_done[s], 1)

            def turned_lo(s, j, layer, b):
                dve.wait_ge(hTh_done[s], hTh_done.at(j, 2 * (layer // 2) + b + 1))
                dve.scalar_tensor_tensor(hT[s][1][:, 2 * b:2 * b + 2, :], bank[s][b][:], 0.0,
                                         hT[s][0][:, 2 * b:2 * b + 2, :], ALU.max, ALU.subtract).then_inc(hTl_done[s], 1)

            def project_lo(which):
                def step(s, j, layer, half):
                    z, b0, k = (zg, 2, 0) if which == "grav" else (zl, 0, 2)
                    dve.wait_ge(zh_done[s], zh_done.at(j, 4 * (layer // 2) + k + half + 1))
                    dve.scalar_tensor_tensor(z[s][1][:, 2 * half:2 * half + 2, :], bank[s][b0 + half][:], 1.0 / H_SCALE,
                                             z[s][0][:, 2 * half:2 * half + 2, :],
                                             ALU.mult, ALU.subtract).then_inc(zlo_done[s], 1)
                return step

            def diagonal(s, k, of):
                for nt in range(CT):
                    a = dve.scalar_tensor_tensor(diag[s][:, k, nt, :], bank[s][2 + k][:, nt * (C + P):nt * (C + P) + P],
                                                 1.0, ident[:], ALU.mult, ALU.mult, accum_out=of[s][:, nt:nt + 1])
                return a

            def lang_norms(s, j, layer, n):
                li = layer // 2
                dve.wait_ge(g01_done[s], g01_done.at(j, 2 * li + 2))
                dve_chain.link(dve, diagonal(s, 1, dgl), s, j)
                dve.tensor_scalar(nrm[s][:], dgl[s][:], norm_floor[:, li:li + 1], None, ALU.max).then_inc(dgl_done[s], 1)

            def grav_norms(s, j, layer, n):
                li = layer // 2
                dve.wait_ge(g01_done[s], g01_done.at(j, 2 * li + 1))
                diagonal(s, 0, dgg).then_inc(dgg_done[s], 1)
                dve.wait_ge(dgg_done[s], dgg_done.at(j, li + 1))
                dve.tensor_scalar(bg[s][:], dgg[s][:], neg_c[:, li:li + 1], None, ALU.mult).then_inc(bg_done[s], 1)

            def inverse_degrees(s, j, li, k):
                dve_chain.link(dve, dve.tensor_scalar(deg[s][:, k, :], deg[s][:, k, :], EPS, None, ALU.max), s, j)
                dve_chain.link(dve, dve.reciprocal(deg[s][:, k, :], deg[s][:, k, :]), s, j)
                return dve.tensor_scalar(rdeg[s][:, k, :], deg[s][:, k, :], gates[:, li, k:k + 1], None, ALU.mult)

            def lang_kernel(s, j, layer, n):
                li = layer // 2
                dve.wait_ge(tl_done[s], tl_done.at(j, li + 1))
                row = bank[s][0][:, 0:C].unsqueeze(1).to_broadcast((P, CT, C))
                dve.tensor_tensor(tl[s][:], tl[s][:], row, ALU.mult).then_inc(row_used[s], 1)
                dve.wait_ge(row_used[s], row_used.at(j, li + 1))
                for nt in range(CT):
                    a = dve.scalar_tensor_tensor(Bl[s][:, nt, :], tl[s][:, nt, :], 1.0, adj_off[:, nt, :],
                                                 ALU.mult, ALU.mult, accum_out=deg[s][:, 0, nt:nt + 1])
                dve_chain.link(dve, a, s, j)
                inverse_degrees(s, j, li, 0).then_inc(rdl_done[s], 1)

            def grav_exponent(s, j, layer, n):
                li = layer // 2
                dve.wait_ge(sqr_done[s], sqr_done.at(j, li + 1))
                dve.tensor_tensor(e0[s][:], bank[s][2][:].rearrange("p (t c) -> p t c", t=CT),
                                  sqr[s][:].unsqueeze(1).to_broadcast((P, CT, C)), ALU.add).then_inc(e0_done[s], 1)

            def grav_kernel(s, j, layer, n):
                li = layer // 2
                dve.wait_ge(eg_done[s], eg_done.at(j, li + 1))
                for nt in range(CT):
                    a = dve.scalar_tensor_tensor(Bg[s][:, nt, :], Eg[s][:, nt, :], 1.0, adj_off[:, nt, :],
                                                 ALU.min, ALU.mult, accum_out=deg[s][:, 1, nt:nt + 1])
                dve_chain.link(dve, a, s, j)
                dve_chain.link(dve, inverse_degrees(s, j, li, 1), s, j)

            def mixture(s, j, layer, n):
                li = layer // 2
                dve.wait_ge(kl_done[s], kl_done.at(j, li + 1))
                for nt in range(CT):
                    a = dve.scalar_tensor_tensor(Km[s][:, nt, :], Bg[s][:, nt, :], rdeg[s][:, 1, nt:nt + 1],
                                                 tl[s][:, nt, :], ALU.mult, ALU.add)
                    a.then_inc(K_done[s], 1)

            def values_lo(s, j, layer, half):
                dve.wait_ge(vh_done[s], vh_done.at(j, 2 * (layer // 2) + half + 1))
                dve.scalar_tensor_tensor(vv[s][1][:, half, :], bank[s][1 + half][:], 1.0 / H_SCALE, vv[s][0][:, half, :],
                                         ALU.mult, ALU.subtract).then_inc(vl_done[s], 1)

            def k_lo(s, j, layer, n):
                dve.wait_ge(kth_done[s], kth_done.at(j, layer // 2 + 1))
                dve.tensor_tensor(KT[s][1][:], bank[s][3][:].rearrange("p (t c) -> p t c", t=CT), KT[s][0][:],
                                  ALU.subtract).then_inc(ktl_done[s], 1)

            def add_1_3(s, j, layer, nt):
                li = layer // 2
                done = x2_done if layer == 1 else x4_done
                dve.wait_ge(y_ps[s], y_ps.at(j, (0 if layer == 1 else 4) + nt + 1))
                dve.scalar_tensor_tensor(xs[s][:, nt, :], bank[s][nt][:], v_unscale[:, li:li + 1], xs[s][:, nt, :],
                                         ALU.mult, ALU.add).then_inc(done[s], 1)
                if layer == 3 and nt == CT - 1:
                    dve_chain.end_sample(s)

            def add_2(s, j, layer, mt):
                dve.wait_ge(y_ps[s], y_ps.at(j, 2 + mt + 1))
                dve.wait_ge(xb_done[s], xb_done.at(j, mt + 1))
                dve_chain.link(dve, dve.scalar_tensor_tensor(xs[s][:, mt, :], bank[s][mt][:], l2_unscale[:],
                                                             xb[s][:, mt, :], ALU.mult, ALU.add), s, j)

            prep_steps = [0]

            def link(ins):
                prep_steps[0] += 1
                ins.then_inc(prep_chain, 1)
                dve.wait_ge(prep_chain, prep_steps[0])

            def find_max(s, j, k, n):
                names = SCALE_SETS[k]
                m0 = MATS.index(names[0])
                if k == 0:
                    dve.wait_ge(c_landed, LOADS)
                    dve.tensor_reduce(abs_max[:, 0:1], adj_sb[:].rearrange("p t m -> p (t m)"), AX_X, ALU.max,
                                      apply_absolute_value=True)
                    dve.tensor_reduce(abs_max[:, 1:2], wqk_f[:].rearrange("p t k -> p (t k)"), AX_X, ALU.max,
                                      apply_absolute_value=True).then_inc(max_found, 1)
                    return
                for m, name in enumerate(names, m0):
                    job = [x[2] for x in JOBS].index(name)
                    if JOBS[job][1] == "multiply":
                        dve.wait_ge(copied, copies(job + 1))
                        src = product_f
                    else:
                        dve.wait_ge(w_landed[job % 4], 32 * (job // 4 + 1))
                        src = staging[job % 4]
                    for half in range(2):
                        a = dve.tensor_reduce(part_max[:, m, half:half + 1], src[half].rearrange("p t n -> p (t n)"),
                                              AX_X, ALU.max, apply_absolute_value=True)
                link(a)
                dve.tensor_reduce(abs_max[:, m0:m0 + len(names)], part_max[:, m0:m0 + len(names), :], AX_X,
                                  ALU.max).then_inc(max_found, 1)

            def find_scale(s, j, k, n):
                m0, width = MATS.index(SCALE_SETS[k][0]), len(SCALE_SETS[k])
                a, b = scratch[:, 0, 0:width], scratch[:, 1, 0:width]
                dve.wait_ge(max_row, k + 1)
                rows = bank[1][3][:, 0:width * P].rearrange("p (m c) -> p m c", m=width)
                link(dve.tensor_reduce(a, rows, AX_X, ALU.max))
                link(dve.tensor_scalar(b.bitcast(U32), a.bitcast(U32), 0x7F800000, None, ALU.bitwise_and))
                link(dve.tensor_scalar(inv[:, m0:m0 + width, 0], b, 2.0 ** -100, 1.0 / W_TOP, ALU.max, ALU.mult))
                dve.reciprocal(scale[:, m0:m0 + width, 0], inv[:, m0:m0 + width, 0]).then_inc(scaled, 1)
                dve.wait_ge(scaled, k + 1)

            def adj_square(s, j, layer, n):
                dve.tensor_scalar(Bl[0][:], adj_sb[:], s_of("adj"), None, ALU.mult).then_inc(squared, 1)
                dve.wait_ge(squared, 1)
                dve.tensor_tensor(tl[0][:], Bl[0][:], Bl[0][:], ALU.mult).then_inc(squared, 1)
                dve.tensor_scalar(qk_unscale[:], i_of("qk"), 1.0 / H_SCALE, None, ALU.mult)
                dve.tensor_scalar(l0_unscale[:], i_of("adj"), 1.0 / (PT_SCALE * E_SCALE), None, ALU.mult)
                dve.scalar_tensor_tensor(l2_unscale[:], i_of("adj"), 1.0 / H_SCALE, i_of("adj"), ALU.mult, ALU.mult)

            def adj_split_lo(s, j, layer, n):
                dve.wait_ge(adj_hi, 1)
                dve.scalar_tensor_tensor(wqk[1][:], wqk_f[:], s_of("qk"), wqk[0][:], ALU.mult,
                                         ALU.subtract).then_inc(adj_lo, 1)
                dve.wait_ge(adj_hi, 2)
                dve.scalar_tensor_tensor(adjT[1][:], bank[0][3][:].rearrange("p (t c) -> p t c", t=CT), s_of("adj"),
                                         adjT[0][:], ALU.mult, ALU.subtract).then_inc(adj_lo, 1)
                dve.wait_ge(adj_hi, 3)
                dve.wait_ge(squared, 2)
                dve.tensor_tensor(adj2[1][:], tl[0][:], adj2[0][:], ALU.subtract)

            def matrix_lo(s, j, job, n):
                how, name = JOBS[job][1:]
                hi, lo = weight[name[:-1], int(name[-1])]
                for dt in range(DT):
                    dve.wait_ge(w_hi, splits(job) + dt + 1)
                    src = tile_bank(job * DT + dt)[:] if how == "turn" else product_f[dt // 2][:, dt % 2, :]
                    dve.scalar_tensor_tensor(lo[:, dt, :], src, s_of(name), hi[:, dt, :],
                                             ALU.mult, ALU.subtract).then_inc(w_lo, 1)

            def factors(s, j, layer, n):
                li = layer // 2
                col = slice(li, li + 1)
                dve.wait_ge(consts_made, 5)
                dve.wait_ge(prep_exp, 2)
                link(dve.tensor_scalar(small[:, 4:5], small[:, col], 1.0, None, ALU.add))
                link(dve.reciprocal(small[:, 5:6], small[:, 4:5]))
                dve.tensor_scalar(gates[:, li, 0:1], small[:, 5:6], K_SCALE, None, ALU.mult)
                dve.tensor_scalar(gates[:, li, 1:2], small[:, 5:6], -K_SCALE, K_SCALE, ALU.mult, ALU.add)
                sigma = small[:, 2 + li:3 + li]
                link(dve.scalar_tensor_tensor(small[:, 6:7], sigma, 1.0, sigma, ALU.mult, ALU.mult))
                link(dve.reciprocal(small[:, 7:8], small[:, 6:7]))
                ig = i_of(f"grav{layer}")
                link(dve.scalar_tensor_tensor(small[:, 6:7], ig, small[:, 7:8], ig, ALU.mult, ALU.mult))
                dve.tensor_scalar(two_c[:, col], small[:, 6:7], 1.0, None, ALU.mult)
                dve.tensor_scalar(neg_c[:, col], small[:, 6:7], -0.5, None, ALU.mult)
                sl = s_of(f"lang{layer}")
                dve.scalar_tensor_tensor(norm_floor[:, col], sl, EPS * EPS, sl, ALU.mult, ALU.mult)
                dve.tensor_scalar(v_unscale[:, col], i_of(f"vo{layer}"), 1.0 / K_SCALE, None, ALU.mult)

            run(dve, "dve", {"MX": find_max, "SC": find_scale, "SQ": adj_square, "AD": adj_split_lo, "LO": matrix_lo,
                             "FA": factors,
                             "BS": statistics, "ST": mean_and_variance, "N": normalise, "H": h_lo, "AH": adj_h_lo, "QM": q_max, "Q": q_less,
                             "E": exponentials, "SM": sums, "AT": attended, "X": add_0, "T": turned_lo,
                             "L": project_lo("lang"), "G": project_lo("grav"), "DL": lang_norms, "DG": grav_norms,
                             "RL": lang_kernel, "RG": grav_exponent, "BG": grav_kernel, "K": mixture,
                             "V": values_lo, "KT": k_lo, "Y": add_1_3, "S": add_2})

        @block.gpsimd
        def _(pool):
            def deviations(s, j, layer, n):
                pool.wait_ge(stats_done[s], stats_done.at(j, layer + 1))
                pool.tensor_tensor(rstd[s][:], var_in[s][:], minus_half[:], ALU.pow).then_inc(rstd_done[s], 1)

            def add_bias(s, j, layer, ct):
                pool.tensor_tensor(xb[s][:, ct, :], xs[s][:, ct, :], bias_row[:], ALU.add).then_inc(xb_done[s], 1)

            def sum_e(s, j, layer, n):
                pool.wait_ge(e_done[s], e_done.at(j, 2 * n + 2))
                a = pool.tensor_tensor(esum[s][:, n, :], E[s][:, 2 * n, :], E[s][:, 2 * n + 1, :], ALU.add)
                if n == 1:
                    pool_chain.link(pool, a, s, j)
                    pool.tensor_tensor(esum[s][:, 0, :], esum[s][:, 0, :], esum[s][:, 1, :],
                                       ALU.add).then_inc(esum_done[s], 1)

            def inverse_norms(s, j, layer, n):
                pool.wait_ge(dgl_done[s], dgl_done.at(j, layer // 2 + 1))
                pool.tensor_tensor(rsl[s][:], nrm[s][:], minus_half[:], ALU.pow).then_inc(rsl_done[s], 1)
                if layer == 3:
                    pool_chain.end_sample(s)

            def constants(s, j, layer, n):
                pool.memset(ident[:], 0.0).then_inc(consts_made, 1)
                pool.memset(ones[:], 1.0).then_inc(consts_made, 1)
                pool.memset(minus_half[:], -0.5).then_inc(consts_made, 1)
                pool.wait_ge(consts_made, 3)
                pool.affine_select(out=ident[:], in_=ident[:], compare_op=ALU.not_equal, fill=1.0, base=0,
                                   pattern=[[-1, P]], channel_multiplier=1).then_inc(consts_made, 1)

            def off_diagonal(s, j, layer, n):
                pool.wait_ge(c_landed, LOADS)
                pool.affine_select(out=adj_off[:], in_=adj_sb[:], compare_op=ALU.not_equal, fill=0.0, base=0,
                                   pattern=[[P, CT], [-1, C]], channel_multiplier=1).then_inc(consts_made, 1)

            run(pool, "pool", {"CO": constants, "OF": off_diagonal,
                               "ST": deviations, "XB": add_bias, "SE": sum_e, "DL": inverse_norms})


_INS = ["x", "adj", "L0_gnn_wq", "L0_gnn_wk", "L0_gnn_bm",
        "L1_gnn_W_lang", "L1_gnn_W_grav", "L1_gnn_W_V", "L1_gnn_W_O", "L1_gnn_gate_logit", "L1_gnn_log_sigma",
        "L2_gnn_bias",
        "L3_gnn_W_lang", "L3_gnn_W_grav", "L3_gnn_W_V", "L3_gnn_W_O", "L3_gnn_gate_logit", "L3_gnn_log_sigma"]


def kernel(**inputs):
    import numpy as _np
    import concourse.bacc as _bacc
    from concourse import mybir as _mybir
    from concourse.bass_utils import run_bass_kernel_spmd as _run

    nc = _bacc.Bacc("TRN2", target_bir_lowering=False, num_devices=1)
    arrays, args = {}, []
    for name in _INS:
        a = _np.ascontiguousarray(inputs[name])
        if a.ndim == 0 or a.size == 1:
            a = a.reshape(1, 1)
        arrays[f"in_{name}"] = a
        args.append(nc.dram_tensor(f"in_{name}", a.shape, _mybir.dt.from_np(a.dtype), kind="ExternalInput").ap())
    shape = inputs["x"].shape
    out = nc.dram_tensor("out_0", shape, _mybir.dt.float32, kind="ExternalOutput").ap()
    build(nc, *args, out)
    r = _run(nc, [arrays], core_ids=[0])
    return r.results[0]["out_0"]
```
